# Optimizing a Trainium2 kernel written in Bass

```python
import numpy as np
import jax
import jax.numpy as jnp

def _softmax(x, axis=-1):
    return jax.nn.softmax(x, axis=axis)

def _gelu(x):
    return jax.nn.gelu(x, approximate=True)

def _silu(x):
    return jax.nn.silu(x)

def _sigmoid(x):
    return jax.nn.sigmoid(x)

def _layernorm(x, axis=-1, eps=1e-05):
    m = jnp.mean(x, axis=axis, keepdims=True)
    v = jnp.var(x, axis=axis, keepdims=True)
    return (x - m) / jnp.sqrt(v + eps)

def _scatter_add(tgt, idx, src, axis=0):
    return tgt.at[idx].add(src)

def _segment_sum(src, seg, n):
    return jax.ops.segment_sum(src, seg, n)
kernel_name = 'mk_adj_preln_d4_adj_r2_34a661'

def setup_inputs(seed: int=0):
    np.random.seed(seed)
    _w = jnp.asarray

    def _rec_inputs():
        import jax
        import jax.numpy as jnp
        _gk = jax.random.key(seed)
        x = -0.0005207 + 1.001 * jax.random.normal(jax.random.fold_in(_gk, 1), (4096, 128), jnp.float32)
        _w = (1.0 + jnp.arange(4096, dtype=jnp.float32)) ** (-0.5)
        _w = _w / _w.mean()
        _pij = jnp.clip(0.00390625 * _w[:, None] * _w[None, :], 0.0, 1.0)
        _a = jax.random.uniform(jax.random.fold_in(_gk, 2), (4096, 4096)) < _pij
        _a = jnp.logical_or(_a, jnp.eye(4096, dtype=bool))
        _af = _a.astype(jnp.float32)
        _af = _af * jax.random.uniform(jax.random.fold_in(_gk, 3), (4096, 4096), jnp.float32, 0.05, 1)
        adj = _af
        return (x, adj)
    x, adj = _rec_inputs()

    def _L0_gnn_setup():
        import jax, jax.numpy as jnp
        import numpy as np
        N, DIM = (8192, 128)

        def _gru_cell(x, h, W_ih, W_hh, b_ih, b_hh):
            gi = x @ W_ih.T + b_ih
            gh = h @ W_hh.T + b_hh
            i_r, i_z, i_n = jnp.split(gi, 3, axis=-1)
            h_r, h_z, h_n = jnp.split(gh, 3, axis=-1)
            r = jax.nn.sigmoid(i_r + h_r)
            z = jax.nn.sigmoid(i_z + h_z)
            n = jnp.tanh(i_n + r * h_n)
            return (1.0 - z) * n + z * h
        key = jax.random.key(seed)
        ks = jax.random.split(key, 8)
        states = jax.random.normal(ks[0], (N, DIM), dtype=jnp.float32)
        adj = jax.random.uniform(ks[1], (N, N), dtype=jnp.float32)
        s = 1.0 / np.sqrt(DIM)
        W_msg = jax.random.uniform(ks[2], (DIM, DIM), minval=-s, maxval=s, dtype=jnp.float32)
        b_msg = jax.random.uniform(ks[3], (DIM,), minval=-s, maxval=s, dtype=jnp.float32)
        W_ih = jax.random.uniform(ks[4], (3 * DIM, DIM), minval=-s, maxval=s, dtype=jnp.float32)
        W_hh = jax.random.uniform(ks[5], (3 * DIM, DIM), minval=-s, maxval=s, dtype=jnp.float32)
        b_ih = jax.random.uniform(ks[6], (3 * DIM,), minval=-s, maxval=s, dtype=jnp.float32)
        b_hh = jax.random.uniform(ks[7], (3 * DIM,), minval=-s, maxval=s, dtype=jnp.float32)
        return {'states': states, 'adj': adj, 'W_msg': W_msg, 'b_msg': b_msg, 'W_ih': W_ih, 'W_hh': W_hh, 'b_ih': b_ih, 'b_hh': b_hh}
    _L0_gnn_all = _L0_gnn_setup()
    _L0_gnn_in = {k: v for k, v in _L0_gnn_all.items() if k in ('W_msg', 'b_msg', 'W_ih', 'W_hh', 'b_ih', 'b_hh')}
    del _L0_gnn_all

    def _L1_gnn_setup():
        import jax, jax.numpy as jnp
        import numpy as np
        N = 4096
        IN_DIM = 128
        OUT_DIM = 128
        DENSITY = 0.01
        key = jax.random.key(seed)
        kx, ka, kw, ks, kd = jax.random.split(key, 5)
        x = jax.random.normal(kx, (N, IN_DIM), dtype=jnp.float32) * 0.1
        adj_matrix = (jax.random.uniform(ka, (N, N)) < DENSITY).astype(jnp.float32)
        adj_matrix = jnp.maximum(adj_matrix, jnp.eye(N, dtype=jnp.float32))
        weight = jax.random.normal(kw, (OUT_DIM, IN_DIM), dtype=jnp.float32) * 0.05
        att_src = jax.random.normal(ks, (1, OUT_DIM), dtype=jnp.float32) * 0.1
        att_dst = jax.random.normal(kd, (1, OUT_DIM), dtype=jnp.float32) * 0.1
        return {'x': x, 'adj_matrix': adj_matrix, 'weight': weight, 'att_src': att_src, 'att_dst': att_dst}
    _L1_gnn_all = _L1_gnn_setup()
    _L1_gnn_in = {k: v for k, v in _L1_gnn_all.items() if k in ('weight', 'att_src', 'att_dst')}
    del _L1_gnn_all

    def _L2_gnn_setup():
        import jax, jax.numpy as jnp
        import numpy as np
        N = 4096
        F = 128
        key = jax.random.key(seed)
        k1, k2, k3 = jax.random.split(key, 3)
        x = jax.random.normal(k1, (N, F), dtype=jnp.float32)
        adj = jax.random.uniform(k2, (N, N), dtype=jnp.float32)
        limit = float(np.sqrt(6.0 / (F + F)))
        weight = jax.random.uniform(k3, (F, F), dtype=jnp.float32, minval=-limit, maxval=limit)
        return {'x': x, 'adj': adj, 'weight': weight}
    _L2_gnn_all = _L2_gnn_setup()
    _L2_gnn_in = {k: v for k, v in _L2_gnn_all.items() if k in ('weight',)}
    del _L2_gnn_all

    def _L3_gnn_setup():
        import jax, jax.numpy as jnp
        import numpy as np
        EPS = 1e-05
        MIN_NORM = 1e-15

        def _norm(x):
            return jnp.maximum(jnp.linalg.norm(x, axis=-1, keepdims=True), MIN_NORM)

        def _artanh(x):
            return jnp.arctanh(jnp.clip(x, -1.0 + EPS, 1.0 - EPS))

        def expmap0(u):
            un = _norm(u)
            return jnp.tanh(un) * u / un

        def logmap0(y):
            yn = _norm(y)
            return _artanh(yn) * y / yn

        def mobius_matvec(W, x):
            mx = x @ W
            xn = _norm(x)
            mxn = _norm(mx)
            res = jnp.tanh(mxn / xn * _artanh(xn)) * mx / mxn
            zero = jnp.all(mx == 0.0, axis=-1, keepdims=True)
            return jnp.where(zero, 0.0, res)

        def mobius_scalar_mul(r, x):
            xn = _norm(x)
            return jnp.tanh(r * _artanh(xn)) * x / xn

        def _clamp_abs(x, eps=1e-10):
            return jnp.where(x >= 0.0, jnp.maximum(x, eps), jnp.minimum(x, -eps))
        key = jax.random.key(seed)
        k1, k2, k3 = jax.random.split(key, 3)
        N, D_IN, D_OUT = (4096, 128, 128)
        AVG_DEG = 64.0
        v = 0.1 * jax.random.normal(k1, (N, D_IN), dtype=jnp.float32)
        X = expmap0(v)
        mask = (jax.random.uniform(k2, (N, N)) < AVG_DEG / N).astype(jnp.float32)
        mask = mask + jnp.eye(N, dtype=jnp.float32)
        A_hat = mask / mask.sum(-1, keepdims=True)
        W = jax.random.uniform(k3, (D_IN, D_OUT), dtype=jnp.float32)
        return {'X': X, 'A_hat': A_hat, 'W': W}
    _L3_gnn_all = _L3_gnn_setup()
    _L3_gnn_in = {k: v for k, v in _L3_gnn_all.items() if k in ('W',)}
    del _L3_gnn_all
    return {'x': x, 'adj': adj, 'L0_gnn_W_msg': _L0_gnn_in['W_msg'], 'L0_gnn_b_msg': _L0_gnn_in['b_msg'], 'L0_gnn_W_ih': _L0_gnn_in['W_ih'], 'L0_gnn_W_hh': _L0_gnn_in['W_hh'], 'L0_gnn_b_ih': _L0_gnn_in['b_ih'], 'L0_gnn_b_hh': _L0_gnn_in['b_hh'], 'L1_gnn_weight': _L1_gnn_in['weight'], 'L1_gnn_att_src': _L1_gnn_in['att_src'], 'L1_gnn_att_dst': _L1_gnn_in['att_dst'], 'L2_gnn_weight': _L2_gnn_in['weight'], 'L3_gnn_W': _L3_gnn_in['W']}

def reference(x, adj, L0_gnn_W_msg, L0_gnn_b_msg, L0_gnn_W_ih, L0_gnn_W_hh, L0_gnn_b_ih, L0_gnn_b_hh, L1_gnn_weight, L1_gnn_att_src, L1_gnn_att_dst, L2_gnn_weight, L3_gnn_W):
    import jax
    import jax.numpy as jnp

    def _L0_gnn_ref(states, adj, W_msg, b_msg, W_ih, W_hh, b_ih, b_hh):
        import jax, jax.numpy as jnp
        import numpy as np
        N, DIM = (8192, 128)

        def _gru_cell(x, h, W_ih, W_hh, b_ih, b_hh):
            gi = x @ W_ih.T + b_ih
            gh = h @ W_hh.T + b_hh
            i_r, i_z, i_n = jnp.split(gi, 3, axis=-1)
            h_r, h_z, h_n = jnp.split(gh, 3, axis=-1)
            r = jax.nn.sigmoid(i_r + h_r)
            z = jax.nn.sigmoid(i_z + h_z)
            n = jnp.tanh(i_n + r * h_n)
            return (1.0 - z) * n + z * h
        agg = adj @ states
        msg = jax.nn.relu(agg @ W_msg.T + b_msg)
        return _gru_cell(msg, states, W_ih, W_hh, b_ih, b_hh)

    def _L1_gnn_ref(x, adj_matrix, weight, att_src, att_dst):
        import jax, jax.numpy as jnp
        import numpy as np
        N = 4096
        IN_DIM = 128
        OUT_DIM = 128
        DENSITY = 0.01
        H = x @ weight.T
        alpha_src = jnp.sum(H * att_src[0], axis=-1)
        alpha_dst = jnp.sum(H * att_dst[0], axis=-1)
        C = alpha_src[None, :] + alpha_dst[:, None]
        Tau = adj_matrix.T * jnp.exp(jnp.maximum(0.2 * C, C))
        att_weights = Tau / jnp.sum(Tau, axis=1, keepdims=True)
        Z = adj_matrix.T * att_weights @ H
        return Z

    def _L2_gnn_ref(x, adj, weight):
        import jax, jax.numpy as jnp
        import numpy as np
        N = 4096
        F = 128
        n = adj.shape[0]
        adj_hat = adj + jnp.eye(n, dtype=adj.dtype)
        deg = jnp.sum(adj_hat, axis=1)
        d_inv_sqrt = (deg + 1e-08) ** (-0.5)
        support = d_inv_sqrt[:, None] * adj_hat * d_inv_sqrt[None, :]
        out = jnp.matmul(jnp.matmul(support, x), weight)
        return jax.nn.relu(out)

    def _L3_gnn_ref(X, A_hat, W):
        import jax, jax.numpy as jnp
        import numpy as np
        EPS = 1e-05
        MIN_NORM = 1e-15

        def _norm(x):
            return jnp.maximum(jnp.linalg.norm(x, axis=-1, keepdims=True), MIN_NORM)

        def _artanh(x):
            return jnp.arctanh(jnp.clip(x, -1.0 + EPS, 1.0 - EPS))

        def expmap0(u):
            un = _norm(u)
            return jnp.tanh(un) * u / un

        def logmap0(y):
            yn = _norm(y)
            return _artanh(yn) * y / yn

        def mobius_matvec(W, x):
            mx = x @ W
            xn = _norm(x)
            mxn = _norm(mx)
            res = jnp.tanh(mxn / xn * _artanh(xn)) * mx / mxn
            zero = jnp.all(mx == 0.0, axis=-1, keepdims=True)
            return jnp.where(zero, 0.0, res)

        def mobius_scalar_mul(r, x):
            xn = _norm(x)
            return jnp.tanh(r * _artanh(xn)) * x / xn

        def _clamp_abs(x, eps=1e-10):
            return jnp.where(x >= 0.0, jnp.maximum(x, eps), jnp.minimum(x, -eps))
        XW = mobius_matvec(W, X)
        sq = jnp.sum(XW * XW, axis=-1, keepdims=True)
        gamma = 2.0 / jnp.maximum(1.0 - sq, EPS)
        nominator = A_hat @ (gamma * XW)
        denominator = _clamp_abs(A_hat @ (gamma - 1.0))
        two_mean = nominator / denominator
        m = mobius_scalar_mul(0.5, two_mean)
        r = A_hat.sum(-1, keepdims=True)
        AXW = mobius_scalar_mul(r, m)
        return expmap0(jax.nn.relu(logmap0(AXW)))
    h = jnp.maximum(_layernorm(x, axis=-1), 0.0)
    x = x + _L0_gnn_ref(h, adj, L0_gnn_W_msg, L0_gnn_b_msg, L0_gnn_W_ih, L0_gnn_W_hh, L0_gnn_b_ih, L0_gnn_b_hh)
    h = jnp.maximum(_layernorm(x, axis=-1), 0.0)
    x = x + _L1_gnn_ref(h, adj, L1_gnn_weight, L1_gnn_att_src, L1_gnn_att_dst)
    h = jnp.maximum(_layernorm(x, axis=-1), 0.0)
    x = x + _L2_gnn_ref(h, adj, L2_gnn_weight)
    h = jnp.maximum(_layernorm(x, axis=-1), 0.0)
    x = x + _L3_gnn_ref(h, adj, L3_gnn_W)
    return x

_drawn_inputs = setup_inputs


def setup_inputs(seed=0):
    import zlib

    import numpy as np

    out = dict(_drawn_inputs(seed))
    spreads = {}
    factors = {'L0_gnn_b_msg': 8.0,
     'L0_gnn_b_ih': 3.426,
     'L0_gnn_b_hh': 5.385,
     'L1_gnn_att_src': 3.349,
     'L1_gnn_att_dst': 8.0,
     'L3_gnn_W': 8.0}
    for name, (base, spread) in spreads.items():
        noise = np.random.default_rng([zlib.crc32(name.encode()), seed]).standard_normal(out[name].shape)
        drawn = base * np.exp(spread * noise) if base else spread * noise
        out[name] = jnp.asarray(drawn.astype(out[name].dtype))
    for name, factor in factors.items():
        out[name] = (out[name] * factor).astype(out[name].dtype)
    return out
```

```python
import math

import numpy as np
import concourse.bass as bass
from concourse import mybir
from contextlib import ExitStack

F32 = mybir.dt.float32
F32R = mybir.dt.float32r
ALU = mybir.AluOpType
ACT = mybir.ActivationFunctionType
AX = mybir.AxisListType


def adjacency_stack(nc, x, adj, w_msg, b_msg, w_ih, w_hh, b_ih, b_hh, w_att, att_src, att_dst, w_gcn, w_hyp, out):
    P = 128
    N, D = x.shape
    BLOCKS = N // P
    B = 4
    C = B * P
    GROUPS = N // C
    SLOTS = 4
    TILES = N // C
    LAG = 4
    LN_EPS, EPS, MIN_NORM, CLAMP, DEG_EPS = 1e-5, 1e-5, 1e-15, 1e-10, 1e-8
    TOP = float(np.float32(1.0 - EPS))
    ATANH_MAX = 0.5 * math.log((1.0 + TOP) / (1.0 - TOP))
    L0, L1, L2, L3 = range(4)
    AGG = {L0: 0, L2: 1, L3: 2}

    ctx = ExitStack()
    with ctx:
        def sb(name, shape, dt=F32):
            return ctx.enter_context(nc.sbuf_tensor(name, shape, dt))

        def pb(name):
            return ctx.enter_context(nc.psum_tensor(name, [P, C], F32))

        def sem(name):
            return ctx.enter_context(nc.semaphore(name))

        x_all = sb("x_all", [P, BLOCKS, D])
        src_hi = sb("src_hi", [P, BLOCKS, D], F32R)
        src_lo = sb("src_lo", [P, BLOCKS, D], F32R)
        nat_a = sb("nat_a", [P, BLOCKS, D])
        nat_b = sb("nat_b", [P, BLOCKS, D])
        dst_row = sb("dst_row", [P, N])
        q_pair = sb("q_pair", [P, BLOCKS, P], F32R)
        exp_s = sb("exp_s", [P, BLOCKS])
        exp_ms = sb("exp_ms", [P, BLOCKS])
        deg_part = sb("deg_part", [P, BLOCKS, GROUPS])
        rowsum = sb("rowsum", [P, BLOCKS])
        dinv = sb("dinv", [P, BLOCKS])
        q_all = sb("q_all", [P, BLOCKS])

        ring = sb("ring", [P, SLOTS, B, C])
        t_hi = sb("t_hi", [P, LAG, C], F32R)
        t_lo = sb("t_lo", [P, LAG, C], F32R)
        att_w = sb("att_w", [P, 2, C])
        att_p = sb("att_p", [P, 2, C])
        junk = sb("junk", [P, 2, C], mybir.dt.bfloat16)

        agg_t = sb("agg_t", [P, C])
        msg_t = sb("msg_t", [P, C])
        r_t = sb("r_t", [P, C])
        z_t = sb("z_t", [P, C])
        n_t = sb("n_t", [P, C])
        pre_t = sb("pre_t", [P, C])
        x_new = sb("x_new", [P, B, D])
        h_new = sb("h_new", [P, B, D])
        h_t = sb("h_t", [P, C])
        y_nat = sb("y_nat", [P, B, D])
        tmp = sb("tmp", [P, B, D])
        den_s = sb("den_s", [P, C])
        st6 = sb("st6", [P, B, 6])
        mv = sb("mv", [P, B, 2])
        rstd = sb("rstd", [P, B])
        NSC = 24
        sc = sb("sc", [P, NSC, B])
        SC = {n: sc[:, i, :] for i, n in enumerate(
            ["xn2", "xn", "ss", "mxn", "arg", "ln", "z2", "ser", "mask", "ath", "z", "t", "f", "g", "den",
             "sgn", "c", "un", "k", "one", "inv", "xc", "rec"])}

        ident = sb("ident", [P, P])
        avg32 = sb("avg32", [P, P])
        avg64 = sb("avg64", [P, 1])
        mhalf = sb("mhalf", [P, BLOCKS])
        phalf = sb("phalf", [P, B])
        ln_eps = sb("ln_eps", [P, B])
        minus_one = sb("minus_one", [P, B])
        w_nat = sb("w_nat", [P, 8, D])
        w_t = sb("w_t", [P, 8, D])
        w_gcn_s = sb("w_gcn_s", [P, D])
        w_hyp_s = sb("w_hyp_s", [P, D])
        att_cols = sb("att_cols", [P, 2])
        w_src = sb("w_src", [P, 1])
        w_dst = sb("w_dst", [P, P])
        bias = sb("bias", [P, 7])
        bias_g = sb("bias_g", [P, 2])

        t_ps = [pb(f"t_ps{i}") for i in range(LAG)]
        acc_ps = pb("acc_ps")
        e0, e1, e2 = pb("e0"), pb("e1"), pb("e2")
        den_ps = t_ps[3]
        den3_ps = e2

        def nodes(ps):
            return ps[:, :].rearrange("p (b d) -> p b d", b=B)

        def grp(t, g):
            return t[:, bass.ds(g * B, B), :]

        def cols(t, g):
            return t[:, bass.ds(g * B, B)]

        def wide(col):
            return col.rearrange("p (b o) -> p b o", o=1).to_broadcast([P, B, D])

        x_in, w_in = sem("x_in"), sem("w_in")
        adj_in = [sem(f"adj_in{i}") for i in range(SLOTS)]
        row_summed = sem("row_summed")
        t_ready, hi_ready, lo_ready = sem("t_ready"), sem("hi_ready"), sem("lo_ready")
        w_made, p_made, att_mm = sem("w_made"), sem("p_made"), sem("att_mm")
        acc_done, acc_free, den_free = sem("acc_done"), sem("acc_free"), sem("den_free")
        const_step, const_ready = sem("const_step"), sem("const_ready")
        wt_ps, wt_ready, wv_ps, wv_ready, bias_ready = (sem(n) for n in ("wt_ps", "wt_ready", "wv_ps", "wv_ready", "bias_ready"))
        ln_stats, ln_mv, ln_rstd, ln_scaled, ln_done = (sem(n) for n in ("ln_stats", "ln_mv", "ln_rstd", "ln_scaled", "ln_done"))
        src_ready, src_step = sem("src_ready"), sem("src_step")
        h0_ps, h0_t = sem("h0_ps"), sem("h0_t")
        x_kept, xnew_ready = sem("x_kept"), sem("xnew_ready")
        gh_ps, msg_ps, msg_ready, rz_ps, hn_ps, in_ps = (sem(n) for n in ("gh_ps", "msg_ps", "msg_ready", "rz_ps", "hn_ps", "in_ps"))
        r_tanh, z_tanh, r_ready, z_ready, rh_ready, npre_ready, n_ready = (sem(n) for n in (
            "r_tanh", "z_tanh", "r_ready", "z_ready", "rh_ready", "npre_ready", "n_ready"))
        gru_step, gru_out, gru_nat = sem("gru_step"), sem("gru_out"), sem("gru_nat")
        hT_ps, hT_ready = sem("hT_ps"), sem("hT_ready")
        proj_ps, exps_ready, att_src_ready = sem("proj_ps"), sem("exps_ready"), sem("att_src_ready")
        den_ps_ready, rden_ready, z_norm, z_nat, num_copied = (sem(n) for n in ("den_ps_ready", "rden_ready", "z_norm", "z_nat", "num_copied"))
        deg_done, dinv_step, dinv_ready, rowsum_ready = sem("deg_done"), sem("dinv_step"), sem("dinv_ready"), sem("rowsum_ready")
        self_ready, self_ps, self_t = sem("self_ready"), sem("self_ps"), sem("self_t")
        gcn_ps, gcn_scaled = sem("gcn_ps"), sem("gcn_scaled")
        mx_ps, mx_ready = sem("mx_ps"), sem("mx_ready")
        pool_step = sem("pool_step")
        ln_arg, ln_val, th_arg, th_val = sem("ln_arg"), sem("ln_val"), sem("th_arg"), sem("th_val")
        v_nat, v_ready, den_nat, den_ready = sem("v_nat"), sem("v_ready"), sem("den_nat"), sem("den_ready")
        ln_arg3, ln_val3, th_arg3, th_val3 = sem("ln_arg3"), sem("ln_val3"), sem("th_arg3"), sem("th_val3")
        out_ready, out_stored = sem("out_ready"), sem("out_stored")
        hyp_src_ready = sem("hyp_src_ready")
        scaled_src = sem("scaled_src")
        xn2_ready, u_made, un2_ready = sem("xn2_ready"), sem("u_made"), sem("un2_ready")

        block = ctx.enter_context(nc.Block())

        def passes(engine, body):
            for p in (L0, L1, L2, L3):
                body(p, 0, True)
                with engine.Fori(1, GROUPS) as g:
                    body(p, g, False)

        @block.sync
        def _(sp):
            for b in range(GROUPS):
                sp.dma_start(grp(x_all, b), x[b * C:(b + 1) * C, :].rearrange("(b p) d -> p b d", p=P)).then_inc(x_in, 16)

            def body(p, g, first):
                for k in range(TILES):
                    s, wrap = k % SLOTS, k < SLOTS
                    q = p - 1 if first and wrap else p
                    done = (TILES * GROUPS if first and wrap else TILES * g) + k - SLOTS + 1
                    if q in AGG:
                        sp.wait_ge(t_ready, (AGG[q] * TILES * GROUPS + done) * B)
                    elif q == L1:
                        sp.wait_ge(p_made, done * B)
                        sp.wait_ge(row_summed, done * B)
                    row, col = (k, g) if p == L1 else (g, k)
                    tile = adj[bass.ds(row * C, C), bass.ds(col * C, C)]
                    sp.dma_start(ring[:, s, :, :], tile.rearrange("(b p) c -> p b c", p=P)).then_inc(adj_in[s], 16)
                    if p == L3 and not first and k == TILES - 1:
                        store(g - 1)

            def store(g):
                sp.wait_ge(out_ready, g + 1)
                sp.dma_start(out[bass.ds(g * C, C), :].rearrange("(b p) d -> p b d", p=P), x_new[:, :, :]).then_inc(out_stored, 16)

            sp.sem_inc(out_stored, 16)
            passes(sp, body)
            store(GROUPS - 1)
            sp.wait_ge(out_stored, 16 * (GROUPS + 1))

        def tile_arrived(engine, p, g, k):
            engine.wait_ge(adj_in[k % SLOTS], 16 * ((p * GROUPS + g) * (TILES // SLOTS) + k // SLOTS + 1))

        @block.tensor
        def _(pe):
            pe.wait_ge(w_in, 16 * 11)
            pe.wait_ge(const_ready, 1)
            for i in range(8):
                last = nc.tensor.transpose((e0 if i < 4 else e1)[:, bass.ds((i % 4) * P, P)], w_nat[:, i, :], ident[:, :])
            last.then_inc(wt_ps, 1)
            nc.tensor.matmul(e2[:, 0:1], w_nat[:, 7, :], att_cols[:, 0:1], start=True, stop=True)
            nc.tensor.matmul(e2[:, P:2 * P], w_nat[:, 7, :], att_cols[:, 1:2].to_broadcast([P, P]),
                             start=True, stop=True).then_inc(wv_ps, 1)

            def transpose4(dst, src):
                for b in range(B):
                    last = nc.tensor.transpose(dst[:, b * P:(b + 1) * P], src(b), ident[:, :])
                return last

            def hT(c):
                pe.wait_ge(ln_done, c + 1)
                transpose4(e1, lambda b: h_new[:, b, :]).then_inc(hT_ps, 1)

            def tail0(e, jb):
                if jb == (0 if isinstance(e, int) else LAG):
                    pe.wait_ge(h0_t, GROUPS)
                    hid = nat_b_t(e)
                    nc.tensor.matmul(e0[:, :], w_t[:, 4, :], hid, start=True, stop=False)
                    nc.tensor.matmul(e1[:, :], w_t[:, 5, :], hid, start=True, stop=False)
                if jb == 6:
                    pe.wait_ge(acc_free, e + 1)
                    nc.tensor.matmul(e2[:, :], w_t[:, 0, :], agg_t[:, :], start=True, stop=True).then_inc(msg_ps, 1)
                if jb == 8:
                    pe.wait_ge(msg_ready, e + 1)
                    nc.tensor.matmul(e0[:, :], w_t[:, 1, :], msg_t[:, :], start=False, stop=True).then_inc(rz_ps, 1)
                    nc.tensor.matmul(e1[:, :], w_t[:, 2, :], msg_t[:, :], start=False, stop=True).then_inc(rz_ps, 1)
                if jb == 9:
                    nc.tensor.matmul(e2[:, :], w_t[:, 6, :], nat_b_t(e), start=True, stop=True).then_inc(hn_ps, 1)
                if jb == 12:
                    pe.wait_ge(r_tanh, e + 1)
                    nc.tensor.matmul(e0[:, :], w_t[:, 3, :], msg_t[:, :], start=True, stop=True).then_inc(in_ps, 1)
                if jb == 20:
                    pe.wait_ge(gru_out, e + 1)
                    pe.wait_ge(z_tanh, e + 1)
                    transpose4(e1, lambda b: n_t[:, b * P:(b + 1) * P]).then_inc(gru_nat, 1)
                if jb == 23:
                    hT(GROUPS + e)
                if jb == 25:
                    pe.wait_ge(hT_ready, e + 1)
                    pe.wait_ge(npre_ready, e + 1)
                    for b in range(B):
                        nc.tensor.matmul(e0[:, b * P:(b + 1) * P], h_t[:, b * P:(b + 1) * P], w_t[:, 7, :], start=True, stop=True)
                    nc.tensor.matmul(e1[:, :], w_dst[:, :], h_t[:, :], start=True, stop=True)
                    for b in range(B):
                        last = nc.tensor.matmul(e2[:, b:b + 1], h_t[:, b * P:(b + 1) * P], w_src[:, :], start=True, stop=True)
                    last.then_inc(proj_ps, 1)

            def nat_b_t(e):
                return nat_b[:, bass.ds(e * B, B), :].rearrange("p b d -> p (b d)")

            def tail1(e, jb):
                if jb == 2:
                    pe.wait_ge(den_free, e + 1)
                    nc.tensor.matmul(e0[:, :], avg32[:, :], den_s[:, :], start=True, stop=True).then_inc(den_ps_ready, 1)
                if jb == 7:
                    pe.wait_ge(z_norm, e + 1)
                    transpose4(e1, lambda b: n_t[:, b * P:(b + 1) * P]).then_inc(z_nat, 1)

            def tail2(e, jb):
                if jb == 0:
                    pe.wait_ge(self_ready, e + 1)
                    transpose4(e1, lambda b: tmp[:, b, :]).then_inc(self_ps, 1)
                if jb == 6:
                    pe.wait_ge(acc_free, 2 * GROUPS + e + 1)
                    for b in range(B):
                        last = nc.tensor.matmul(e0[:, b * P:(b + 1) * P], agg_t[:, b * P:(b + 1) * P], w_gcn_s[:, :], start=True, stop=True)
                    last.then_inc(gcn_ps, 1)
                if jb == 12:
                    hT(3 * GROUPS + e)
                if jb == 14:
                    pe.wait_ge(hT_ready, GROUPS + e + 1)
                    for b in range(B):
                        last = nc.tensor.matmul(e0[:, b * P:(b + 1) * P], h_t[:, b * P:(b + 1) * P], w_hyp_s[:, :], start=True, stop=True)
                    last.then_inc(mx_ps, 1)

            def tail3(e, jb):
                if jb == 6:
                    pe.wait_ge(acc_free, 3 * GROUPS + e + 1)
                    transpose4(e0, lambda b: agg_t[:, b * P:(b + 1) * P]).then_inc(v_nat, 1)
                    for b in range(B):
                        last = nc.tensor.matmul(e1[:, b:b + 1], den_s[:, b * P:(b + 1) * P], avg64[:, :], start=True, stop=True)
                    last.then_inc(den_nat, 1)

            TAILS = {L0: tail0, L1: tail1, L2: tail2, L3: tail3}

            def products(p, g, jb):
                unit = (AGG[p] * GROUPS + g) * BLOCKS + jb
                pe.wait_ge(lo_ready, unit + 1)
                if jb == 0 and not (p == L0 and isinstance(g, int)):
                    pe.wait_ge(acc_free, p * GROUPS + g)
                if jb % B == 0 and (jb == BLOCKS - LAG or isinstance(g, int) and g == 0):
                    pe.wait_ge(src_ready, AGG[p] * GROUPS + jb // B + 1)
                b = jb % LAG
                first, last = jb == 0, jb == BLOCKS - 1
                nc.tensor.matmul(acc_ps[:, :], src_hi[:, jb, :], t_hi[:, b, :], start=first, stop=False)
                nc.tensor.matmul(acc_ps[:, :], src_lo[:, jb, :], t_hi[:, b, :], start=False, stop=False)
                if p == L3:
                    nc.tensor.matmul(den3_ps[:, :], q_pair[:, jb, :], t_hi[:, b, :], start=first, stop=False)
                    nc.tensor.matmul(den3_ps[:, :], q_pair[:, jb, :], t_lo[:, b, :], start=False, stop=last)
                mm = nc.tensor.matmul(acc_ps[:, :], src_hi[:, jb, :], t_lo[:, b, :], start=False, stop=last)
                if last:
                    mm.then_inc(acc_done, 1)

            def body(p, g, first):
                if p == L1:
                    for jb in range(BLOCKS):
                        if first:
                            tail0(GROUPS - 1, jb)
                        else:
                            tail1(g - 1, jb)
                        if jb == 0:
                            pe.wait_ge(acc_free, GROUPS + g)
                            if not first:
                                pe.wait_ge(den_free, g)
                        if first and jb % B == 0:
                            pe.wait_ge(att_src_ready, jb // B + 1)
                        pe.wait_ge(p_made, g * BLOCKS + jb + 1)
                        b, q = jb % 2, jb % 4
                        nc.tensor.matmul(acc_ps[:, :], nat_a[:, jb, :], att_p[:, b, :], start=jb == 0, stop=jb == BLOCKS - 1)
                        mm = nc.tensor.matmul(den_ps[32 * q:32 * q + 32, :], exp_s[:, jb:jb + 1].to_broadcast([P, 32]),
                                              att_w[:, b, :], start=jb < 4, stop=jb >= BLOCKS - 4)
                        mm.then_inc(att_mm, 1)
                    return
                for jb in range(BLOCKS):
                    if first:
                        if p == L0:
                            if jb % B == 2:
                                k = jb // B
                                pe.wait_ge(ln_done, k + 1)
                                if k:
                                    pe.wait_ge(h0_t, k)
                                else:
                                    pe.wait_ge(wt_ready, 2)
                                transpose4(e1, lambda b: nat_a[:, k * B + b, :]).then_inc(h0_ps, 1)
                        elif p == L2:
                            tail1(GROUPS - 1, jb)
                        else:
                            tail2(GROUPS - 1, jb)
                    else:
                        TAILS[p](g - 1, jb)
                    if jb >= LAG:
                        products(p, g, jb - LAG)
                    elif not first:
                        products(p, g - 1, BLOCKS - LAG + jb)
                    elif p == L3:
                        products(L2, GROUPS - 1, BLOCKS - LAG + jb)
                    if jb % B == 0:
                        tile_arrived(pe, p, g, jb // B)
                    if p == L2 and first and jb == 3:
                        pe.wait_ge(den_free, GROUPS)
                    for b in range(B):
                        last = nc.tensor.transpose(t_ps[jb % LAG][:, b * P:(b + 1) * P],
                                                   ring[:, (jb // B) % SLOTS, b, (jb % B) * P:(jb % B + 1) * P], ident[:, :])
                    last.then_inc(t_ready, 1)

            def flush(p):
                for jb in range(BLOCKS - LAG, BLOCKS):
                    products(p, GROUPS - 1, jb)

            for p in (L0, L1, L2, L3):
                body(p, 0, True)
                with pe.Fori(1, GROUPS) as g:
                    body(p, g, False)
                if p in (L0, L3):
                    flush(p)
            for jb in range(BLOCKS):
                tail3(GROUPS - 1, jb)

        @block.scalar
        def _(act):
            def load(dst, src):
                act.dma_start(dst, src).then_inc(w_in, 16)

            load(w_nat[:, 0, :], w_msg)
            load(w_nat[:, 1:4, :], w_ih.rearrange("(t p) d -> p t d", p=P))
            load(w_nat[:, 4:7, :], w_hh.rearrange("(t p) d -> p t d", p=P))
            load(w_nat[:, 7, :], w_att)
            load(w_gcn_s[:, :], w_gcn)
            load(w_hyp_s[:, :], w_hyp)
            with nc.allow_non_contiguous_dma(reason="a few hundred floats, one per partition"):
                load(att_cols[:, 0:1], att_src.rearrange("o d -> d o"))
                load(att_cols[:, 1:2], att_dst.rearrange("o d -> d o"))
                load(bias[:, 0:1], b_msg.rearrange("(o d) -> d o", o=1))
                load(bias[:, 1:4], b_ih.rearrange("(t d) -> d t", t=3))
                load(bias[:, 4:7], b_hh.rearrange("(t d) -> d t", t=3))
            act.wait_ge(wt_ps, 1)
            nc.scalar.activation(w_t[:, 0:4, :], nodes(e0), ACT.Copy).then_inc(wt_ready, 1)
            nc.scalar.activation(w_t[:, 4:8, :], nodes(e1), ACT.Copy).then_inc(wt_ready, 1)
            act.wait_ge(wv_ps, 1)
            nc.scalar.activation(w_src[:, :], e2[:, 0:1], ACT.Copy).then_inc(wv_ready, 1)
            nc.scalar.activation(w_dst[:, :], e2[:, P:2 * P], ACT.Copy).then_inc(wv_ready, 1)

            def hT(c):
                act.wait_ge(hT_ps, c + 1)
                nc.scalar.activation(h_t[:, :], e1[:, :], ACT.Copy).then_inc(hT_ready, 1)

            def tail0(e, jb):
                if jb == 7:
                    act.wait_ge(msg_ps, e + 1)
                    nc.scalar.activation(msg_t[:, :], e2[:, :], ACT.Relu, bias=bias[:, 0:1]).then_inc(msg_ready, 1)
                if jb == 10:
                    act.wait_ge(rz_ps, 2 * e + 1)
                    nc.scalar.activation(r_t[:, :], e0[:, :], ACT.Tanh, bias=bias_g[:, 0:1], scale=0.5).then_inc(r_tanh, 1)
                if jb == 11:
                    act.wait_ge(rz_ps, 2 * e + 2)
                    nc.scalar.activation(z_t[:, :], e1[:, :], ACT.Tanh, bias=bias_g[:, 1:2], scale=0.5).then_inc(z_tanh, 1)
                if jb == 15:
                    act.wait_ge(npre_ready, e + 1)
                    nc.scalar.activation(n_t[:, :], pre_t[:, :], ACT.Tanh, bias=bias[:, 3:4]).then_inc(n_ready, 1)
                if jb == 24:
                    hT(e)
                if jb == 26:
                    act.wait_ge(proj_ps, e + 1)
                    nc.scalar.activation(cols(exp_s, e), e2[:, 0:B], ACT.Exp).then_inc(exps_ready, 1)
                    nc.scalar.activation(cols(exp_ms, e), e2[:, 0:B], ACT.Exp, scale=-0.8).then_inc(exps_ready, 1)
                    nc.scalar.activation(dst_row[:, bass.ds(e * C, C)], e1[:, :], ACT.Exp, scale=0.8).then_inc(exps_ready, 1)

            def tail1(e, jb):
                pass

            def squares(dst, src):
                for b in range(B):
                    last = nc.scalar.activation(junk[:, 0, b * D:(b + 1) * D], src[:, b, :], ACT.Square, accum_out=SC[dst][:, b:b + 1])
                return last

            def tail2(e, jb):
                if jb == 1:
                    act.wait_ge(self_ps, e + 1)
                    nc.scalar.activation(pre_t[:, :], e1[:, :], ACT.Copy).then_inc(self_t, 1)
                if jb == 12:
                    act.wait_ge(ln_done, 3 * GROUPS + e + 1)
                    squares("xn2", h_new).then_inc(xn2_ready, 1)
                if jb == 13:
                    hT(GROUPS + e)
                if jb == 15:
                    act.wait_ge(mx_ps, e + 1)
                    nc.scalar.activation(y_nat[:, :, :], nodes(e0), ACT.Copy)
                    squares("ss", nodes(e0)).then_inc(mx_ready, 1)
                if jb == 19:
                    act.wait_ge(ln_arg, e + 1)
                    nc.scalar.activation(SC["ln"], SC["arg"], ACT.Ln).then_inc(ln_val, 1)
                if jb == 22:
                    act.wait_ge(th_arg, e + 1)
                    nc.scalar.activation(SC["t"], SC["z"], ACT.Tanh).then_inc(th_val, 1)

            def tail3(e, jb):
                if jb == 7:
                    act.wait_ge(v_nat, e + 1)
                    nc.scalar.activation(y_nat[:, :, :], nodes(e0), ACT.Copy)
                    squares("ss", nodes(e0)).then_inc(v_ready, 1)
                if jb == 15:
                    act.wait_ge(ln_arg3, e + 1)
                    nc.scalar.activation(SC["ln"], SC["arg"], ACT.Ln).then_inc(ln_val3, 1)
                if jb == 19:
                    act.wait_ge(u_made, e + 1)
                    squares("ss", h_new).then_inc(un2_ready, 1)
                if jb == 22:
                    act.wait_ge(th_arg3, e + 1)
                    nc.scalar.activation(SC["t"], SC["un"], ACT.Tanh).then_inc(th_val3, 1)

            TAILS = {L0: tail0, L1: tail1, L2: tail2, L3: tail3}

            def body(p, g, first):
                for jb in range(BLOCKS):
                    if first and p:
                        TAILS[p - 1](GROUPS - 1, jb)
                    elif not first:
                        TAILS[p](g - 1, jb)
                    if p == L1:
                        if jb % B == 0:
                            tile_arrived(act, p, g, jb // B)
                        if not (first and jb < 2):
                            act.wait_ge(row_summed, g * BLOCKS + jb - 1)
                        nc.scalar.activation(junk[:, jb % 2, :], ring[:, (jb // B) % SLOTS, jb % B, :], ACT.Copy,
                                             accum_out=deg_part[:, jb, bass.ds(g, 1)]).then_inc(row_summed, 1)
                        continue
                    act.wait_ge(t_ready, (AGG[p] * GROUPS + g) * BLOCKS + jb + 1)
                    nc.scalar.activation(t_hi[:, jb % LAG, :], t_ps[jb % LAG][:, :], ACT.Copy).then_inc(hi_ready, 1)
                    if p == L0 and first and jb % B == 3:
                        k = jb // B
                        act.wait_ge(h0_ps, k + 1)
                        nc.scalar.activation(nat_b[:, k * B:(k + 1) * B, :], nodes(e1), ACT.Copy).then_inc(h0_t, 1)

            passes(act, body)
            for jb in range(BLOCKS):
                tail3(GROUPS - 1, jb)

        @block.vector
        def _(dve):
            def stats(c, src):
                for b in range(B):
                    last = nc.vector.bn_stats(st6[:, b, :], src(b))
                dve.drain()
                for b in range(B):
                    last = nc.vector.bn_aggr(mv[:, b, :], st6[:, b, :])
                last.then_inc(ln_mv, 1)

            def normalise(c, src, dst):
                dve.wait_ge(ln_rstd, c + 1)
                for b in range(B):
                    last = nc.vector.tensor_scalar(h_new[:, b, :], src(b), mv[:, b, 0:1], rstd[:, b:b + 1], ALU.subtract, ALU.mult)
                last.then_inc(ln_scaled, 1)
                dve.wait_ge(ln_scaled, c + 1)
                nc.vector.tensor_scalar(dst, h_new[:, :, :], 0.0, None, ALU.max).then_inc(ln_done, 1)

            def tail0(e, jb):
                if jb == (0 if isinstance(e, int) else LAG):
                    dve.wait_ge(acc_done, e + 1)
                    nc.vector.tensor_copy(agg_t[:, :], acc_ps[:, :]).then_inc(acc_free, 1)
                if jb == 11:
                    dve.wait_ge(r_tanh, e + 1)
                    nc.vector.tensor_scalar(r_t[:, :], r_t[:, :], 0.5, 0.5, ALU.mult, ALU.add).then_inc(r_ready, 1)
                if jb == 12:
                    dve.wait_ge(r_ready, e + 1)
                    dve.wait_ge(hn_ps, e + 1)
                    nc.vector.scalar_tensor_tensor(pre_t[:, :], e2[:, :], bias[:, 6:7], r_t[:, :], ALU.add, ALU.mult).then_inc(rh_ready, 1)
                if jb == 13:
                    dve.wait_ge(z_tanh, e + 1)
                    nc.vector.tensor_scalar(z_t[:, :], z_t[:, :], 0.5, 0.5, ALU.mult, ALU.add).then_inc(z_ready, 1)
                if jb == 14:
                    dve.wait_ge(rh_ready, e + 1)
                    dve.wait_ge(in_ps, e + 1)
                    nc.vector.tensor_tensor(pre_t[:, :], e0[:, :], pre_t[:, :], ALU.add).then_inc(npre_ready, 1)
                if jb == 21:
                    dve.wait_ge(gru_nat, e + 1)
                    nc.vector.tensor_tensor(x_new[:, :, :], nodes(e1), grp(x_all, e), ALU.add).then_inc(xnew_ready, 1)
                    dve.wait_ge(xnew_ready, e + 1)
                    stats(GROUPS + e, lambda b: x_new[:, b, :])
                if jb == 22:
                    normalise(GROUPS + e, lambda b: x_new[:, b, :], h_new[:, :, :])
                if jb == 27:
                    dve.wait_ge(exps_ready, 3 * e + 3)
                    nc.vector.tensor_tensor(grp(nat_a, e), nodes(e0), wide(cols(exp_s, e)), ALU.mult).then_inc(att_src_ready, 1)

            def tail1(e, jb):
                if jb == 0:
                    dve.wait_ge(att_mm, (e + 1) * BLOCKS)
                    nc.vector.tensor_copy(agg_t[:, :], acc_ps[:, :]).then_inc(acc_free, 1)
                    nc.vector.tensor_copy(den_s[:, :], den_ps[:, :]).then_inc(den_free, 1)
                if jb == 3:
                    dve.wait_ge(den_ps_ready, e + 1)
                    nc.vector.reciprocal(r_t[:, :], e0[:, :]).then_inc(rden_ready, 1)
                if jb == 8:
                    dve.wait_ge(z_nat, e + 1)
                    nc.vector.tensor_tensor(x_new[:, :, :], nodes(e1), grp(x_all, e), ALU.add).then_inc(xnew_ready, 1)
                    dve.wait_ge(xnew_ready, GROUPS + e + 1)
                    stats(2 * GROUPS + e, lambda b: x_new[:, b, :])
                if jb == 10:
                    normalise(2 * GROUPS + e, lambda b: x_new[:, b, :], grp(nat_b, e))

            def tail2(e, jb):
                if jb == 4:
                    dve.wait_ge(acc_done, GROUPS + e + 1)
                    dve.wait_ge(self_t, e + 1)
                    nc.vector.tensor_tensor(agg_t[:, :], acc_ps[:, :], pre_t[:, :], ALU.add).then_inc(acc_free, 1)
                if jb == 8:
                    dve.wait_ge(gcn_ps, e + 1)
                    nc.vector.tensor_tensor(h_new[:, :, :], nodes(e0), wide(cols(dinv, e)), ALU.mult).then_inc(gcn_scaled, 1)
                    dve.wait_ge(gcn_scaled, e + 1)
                    nc.vector.scalar_tensor_tensor(x_new[:, :, :], h_new[:, :, :], 0.0, grp(x_all, e), ALU.max, ALU.add).then_inc(xnew_ready, 1)
                    dve.wait_ge(xnew_ready, 2 * GROUPS + e + 1)
                    stats(3 * GROUPS + e, lambda b: x_new[:, b, :])
                if jb == 10:
                    normalise(3 * GROUPS + e, lambda b: x_new[:, b, :], h_new[:, :, :])

            def tail3(e, jb):
                if jb == 4:
                    dve.wait_ge(acc_done, 2 * GROUPS + e + 1)
                    nc.vector.tensor_copy(den_s[:, :], den3_ps[:, :])
                    nc.vector.tensor_copy(agg_t[:, :], acc_ps[:, :]).then_inc(acc_free, 1)
                if jb == 8:
                    dve.wait_ge(den_nat, e + 1)
                    nc.vector.tensor_copy(SC["den"], e1[:, 0:B]).then_inc(den_ready, 1)

            TAILS = {L0: tail0, L1: tail1, L2: tail2, L3: tail3}

            def body(p, g, first):
                for jb in range(BLOCKS):
                    if first and p:
                        TAILS[p - 1](GROUPS - 1, jb)
                    elif not first:
                        TAILS[p](g - 1, jb)
                    if p == L1:
                        unit = g * BLOCKS + jb
                        if jb % B == 0:
                            tile_arrived(dve, p, g, jb // B)
                            if first:
                                dve.wait_ge(exps_ready, 3 * (jb // B + 1))
                        if not (first and jb < 2):
                            dve.wait_ge(att_mm, unit - 1)
                        tile = ring[:, (jb // B) % SLOTS, jb % B, :]
                        nc.vector.scalar_tensor_tensor(att_w[:, jb % 2, :], dst_row[:, bass.ds(g * C, C)], exp_ms[:, jb:jb + 1], tile,
                                                       ALU.max, ALU.mult).then_inc(w_made, 1)
                        dve.wait_ge(w_made, unit + 1)
                        ins = nc.vector.tensor_tensor(att_p[:, jb % 2, :], att_w[:, jb % 2, :], tile, ALU.mult)
                        ins.then_inc(p_made, 1)
                        continue
                    if p == L2 and first and jb == 0:
                        dve.wait_ge(row_summed, BLOCKS * GROUPS)
                        nc.vector.tensor_reduce(rowsum[:, :], deg_part[:, :, :], AX.X, ALU.add).then_inc(rowsum_ready, 1)
                    dve.wait_ge(hi_ready, (AGG[p] * GROUPS + g) * BLOCKS + jb + 1)
                    nc.vector.tensor_tensor(t_lo[:, jb % LAG, :], t_ps[jb % LAG][:, :], t_hi[:, jb % LAG, :].bitcast(F32),
                                            ALU.subtract).then_inc(lo_ready, 1)
                    if p == L0 and first and jb % B == 0 and jb // B + 2 < GROUPS:
                        layer0_norm(jb // B + 2)

            def layer0_norm(k):
                dve.wait_ge(x_in, 16 * GROUPS)
                stats(k, lambda b: x_all[:, k * B + b, :])
                normalise(k, lambda b: x_all[:, k * B + b, :], nat_a[:, k * B:(k + 1) * B, :])

            layer0_norm(0)
            layer0_norm(1)
            dve.wait_ge(w_in, 16 * 11)
            nc.vector.tensor_tensor(bias_g[:, :], bias[:, 1:3], bias[:, 4:6], ALU.add).then_inc(bias_ready, 1)
            dve.wait_ge(bias_ready, 1)
            nc.vector.tensor_scalar(bias_g[:, :], bias_g[:, :], 0.5, None, ALU.mult).then_inc(bias_ready, 1)
            passes(dve, body)
            for jb in range(BLOCKS):
                tail3(GROUPS - 1, jb)

        @block.gpsimd
        def _(pool):
            g_ = nc.gpsimd
            g_.memset(ident[:, :], 0.0).then_inc(const_step, 1)
            pool.wait_ge(const_step, 1)
            g_.affine_select(out=ident[:, :], in_=ident[:, :], compare_op=ALU.not_equal, fill=1.0, base=0,
                             pattern=[[-1, P]], channel_multiplier=1).then_inc(const_ready, 1)
            g_.memset(avg32[:, :], 1.0 / 32)
            g_.memset(avg64[:, :], 1.0 / 64)
            g_.memset(phalf[:, :], 0.5)
            g_.memset(ln_eps[:, :], LN_EPS)
            g_.memset(minus_one[:, :], -1.0)
            g_.memset(mhalf[:, :], -0.5).then_inc(const_ready, 1)
            pool.wait_ge(const_ready, 2)

            def chain(ins):
                pool.drain()

            def layer_rstd(c, chain):
                pool.wait_ge(ln_mv, c + 1)
                chain(g_.tensor_tensor(rstd[:, :], mv[:, :, 1], ln_eps[:, :], ALU.add))
                g_.tensor_tensor(rstd[:, :], rstd[:, :], phalf_neg, ALU.pow).then_inc(ln_rstd, 1)

            phalf_neg = mhalf[:, 0:B]

            def split(p, k, chain):
                blk = slice(k * B, (k + 1) * B)
                nat = nat_b if p == L2 else nat_a
                if p == L0:
                    pool.wait_ge(ln_done, k + 1)
                if p == L2:
                    pool.wait_ge(ln_done, 2 * GROUPS + k + 1)
                    g_.tensor_tensor(nat[:, blk, :], nat[:, blk, :], wide(dinv[:, blk]), ALU.mult).then_inc(scaled_src, 1)
                    pool.wait_ge(scaled_src, k + 1)
                if p == L3:
                    pool.wait_ge(t_ready, (AGG[L2] * GROUPS + GROUPS - 1) * BLOCKS + (k + 1) * B + LAG)
                chain(g_.tensor_copy(src_hi[:, blk, :], nat[:, blk, :]))
                if p == L3:
                    q = q_all[:, blk].rearrange("p (b o) -> p b o", o=1).to_broadcast([P, B, 64])
                    chain(g_.tensor_copy(q_pair[:, blk, 0:64], q))
                    g_.tensor_tensor(q_pair[:, blk, 64:128], q, q_pair[:, blk, 0:64].bitcast(F32), ALU.subtract)
                g_.tensor_tensor(src_lo[:, blk, :], nat[:, blk, :], src_hi[:, blk, :].bitcast(F32), ALU.subtract).then_inc(src_ready, 1)

            def keep_x(e):
                g_.tensor_copy(grp(x_all, e), x_new[:, :, :]).then_inc(x_kept, 1)

            def tail0(e, chain):
                pool.wait_ge(z_ready, e + 1)
                pool.wait_ge(n_ready, e + 1)
                hid = nat_b[:, bass.ds(e * B, B), :].rearrange("p b d -> p (b d)")
                chain(g_.tensor_tensor(msg_t[:, :], hid, n_t[:, :], ALU.subtract))
                chain(g_.tensor_tensor(msg_t[:, :], msg_t[:, :], z_t[:, :], ALU.mult))
                g_.tensor_tensor(n_t[:, :], n_t[:, :], msg_t[:, :], ALU.add).then_inc(gru_out, 1)
                layer_rstd(GROUPS + e, chain)
                keep_x(e)

            def tail1(e, chain):
                pool.wait_ge(rden_ready, e + 1)
                g_.tensor_tensor(n_t[:, :], agg_t[:, :], r_t[:, :], ALU.mult).then_inc(z_norm, 1)

            def tail1_norm(e, chain):
                layer_rstd(2 * GROUPS + e, chain)
                keep_x(e)

            def ts(chain, dst, a, s1, s2, o1, o2=None):
                chain(g_.tensor_scalar(SC[dst], SC[a], s1, s2, o1, o2) if o2 is not None else
                      g_.tensor_scalar(SC[dst], SC[a], s1, None, o1))

            def tt(chain, dst, a, b, op):
                chain(g_.tensor_tensor(SC[dst], SC[a], SC[b], op))

            def divide(chain, dst, a, b):
                chain(g_.tensor_tensor(SC["rec"], SC[b], minus_one[:, :], ALU.pow))
                tt(chain, dst, a, "rec", ALU.mult)

            def artanh_arg(chain, src):
                ts(chain, "xc", src, 1.0 - EPS, -1.0 + EPS, ALU.min, ALU.max)
                ts(chain, "inv", "xc", -1.0, 1.0, ALU.mult, ALU.add)
                ts(chain, "one", "xc", 1.0, None, ALU.add)
                divide(chain, "arg", "one", "inv")

            def artanh_end(chain):
                tt(chain, "z2", "xc", "xc", ALU.mult)
                ts(chain, "ser", "z2", 1.0 / 7, 1.0 / 5, ALU.mult, ALU.add)
                tt(chain, "ser", "ser", "z2", ALU.mult)
                ts(chain, "ser", "ser", 1.0 / 3, None, ALU.add)
                tt(chain, "ser", "ser", "z2", ALU.mult)
                ts(chain, "ser", "ser", 1.0, None, ALU.add)
                tt(chain, "ser", "ser", "xc", ALU.mult)
                ts(chain, "ath", "ln", 0.5, None, ALU.mult)
                tt(chain, "ser", "ser", "ath", ALU.subtract)
                ts(chain, "mask", "xc", 1.0 / 16, None, ALU.is_lt)
                tt(chain, "ser", "ser", "mask", ALU.mult)
                tt(chain, "ath", "ath", "ser", ALU.add)

            def self_term(e):
                g_.tensor_copy(tmp[:, :, :], grp(nat_b, e)).then_inc(self_ready, 1)

            def tail2_norm(e, chain):
                layer_rstd(3 * GROUPS + e, chain)
                keep_x(e)

            def tail2a(e, chain):
                pool.wait_ge(xn2_ready, e + 1)
                chain(g_.tensor_tensor(SC["xn"], SC["xn2"], phalf[:, :], ALU.pow))
                ts(chain, "xn", "xn", MIN_NORM, None, ALU.max)
                artanh_arg(chain, "xn")
                g_.tensor_copy(SC["arg"], SC["arg"]).then_inc(ln_arg, 1)

            def tail2b(e, chain):
                pool.wait_ge(mx_ready, e + 1)
                chain(g_.tensor_tensor(SC["mxn"], SC["ss"], phalf[:, :], ALU.pow))
                ts(chain, "mxn", "mxn", MIN_NORM, None, ALU.max)
                pool.wait_ge(ln_val, e + 1)
                artanh_end(chain)
                divide(chain, "z", "mxn", "xn")
                tt(chain, "z", "z", "ath", ALU.mult)
                g_.tensor_copy(SC["z"], SC["z"]).then_inc(th_arg, 1)

            def tail2c(e, chain):
                pool.wait_ge(th_val, e + 1)
                divide(chain, "f", "t", "mxn")
                tt(chain, "g", "f", "f", ALU.mult)
                tt(chain, "g", "g", "ss", ALU.mult)
                ts(chain, "g", "g", -1.0, 1.0, ALU.mult, ALU.add)
                ts(chain, "g", "g", EPS, None, ALU.max)
                ts(chain, "g", "g", 0.5, None, ALU.mult)
                chain(g_.tensor_tensor(SC["g"], SC["g"], minus_one[:, :], ALU.pow))
                ts(chain, "c", "g", -1.0, None, ALU.add)
                chain(g_.tensor_copy(cols(q_all, e), SC["c"]))
                tt(chain, "f", "f", "g", ALU.mult)
                g_.tensor_tensor(grp(nat_a, e), y_nat[:, :, :], wide(SC["f"]), ALU.mult).then_inc(hyp_src_ready, 1)

            def tail3(e, chain):
                pool.wait_ge(v_ready, e + 1)
                pool.wait_ge(den_ready, e + 1)
                chain(g_.tensor_tensor(SC["mxn"], SC["ss"], phalf[:, :], ALU.pow))
                ts(chain, "sgn", "den", 0.0, None, ALU.is_ge)
                ts(chain, "sgn", "sgn", 2.0, -1.0, ALU.mult, ALU.add)
                tt(chain, "den", "den", "sgn", ALU.mult)
                ts(chain, "den", "den", CLAMP, None, ALU.max)
                divide(chain, "xn", "mxn", "den")
                ts(chain, "xn", "xn", MIN_NORM, None, ALU.max)
                artanh_arg(chain, "xn")
                g_.tensor_copy(SC["arg"], SC["arg"]).then_inc(ln_arg3, 1)
                tt(chain, "den", "den", "xn", ALU.mult)
                pool.wait_ge(ln_val3, e + 1)
                artanh_end(chain)
                ts(chain, "ath", "ath", 0.5, None, ALU.mult)
                chain(g_.tensor_tensor(SC["ath"], SC["ath"], cols(rowsum, e), ALU.mult))
                ts(chain, "ath", "ath", ATANH_MAX, -ATANH_MAX, ALU.min, ALU.max)
                divide(chain, "c", "ath", "den")
                tt(chain, "c", "c", "sgn", ALU.mult)
                chain(g_.tensor_tensor(h_new[:, :, :], y_nat[:, :, :], wide(SC["c"]), ALU.mult))
                g_.tensor_scalar(h_new[:, :, :], h_new[:, :, :], 0.0, None, ALU.max).then_inc(u_made, 1)
                pool.wait_ge(un2_ready, e + 1)
                chain(g_.tensor_tensor(SC["un"], SC["ss"], phalf[:, :], ALU.pow))
                ts(chain, "un", "un", MIN_NORM, None, ALU.max)
                g_.tensor_copy(SC["un"], SC["un"]).then_inc(th_arg3, 1)
                pool.wait_ge(th_val3, e + 1)
                divide(chain, "k", "t", "un")
                chain(g_.tensor_tensor(h_new[:, :, :], h_new[:, :, :], wide(SC["k"]), ALU.mult))
                pool.wait_ge(out_stored, 16 * (e + 1))
                g_.tensor_tensor(x_new[:, :, :], h_new[:, :, :], grp(x_all, e), ALU.add).then_inc(out_ready, 1)

            def tail2(e, chain):
                self_term(e)
                tail2_norm(e, chain)
                tail2a(e, chain)
                tail2b(e, chain)
                tail2c(e, chain)

            def looped(tail):
                with pool.Fori(0, GROUPS - 1) as e:
                    tail(e, chain)

            for k in range(GROUPS):
                layer_rstd(k, chain)
                split(L0, k, chain)
            looped(tail0)
            tail0(GROUPS - 1, chain)
            looped(lambda e, chain: (tail1(e, chain), tail1_norm(e, chain)))
            def degrees(chain):
                pool.wait_ge(rowsum_ready, 1)
                chain(g_.tensor_scalar(dinv[:, :], rowsum[:, :], 1.0, DEG_EPS, ALU.add, ALU.add))
                chain(g_.tensor_tensor(dinv[:, :], dinv[:, :], mhalf[:, :], ALU.pow))
            degrees(chain)
            last = GROUPS - 1
            split(L2, 0, chain)
            tail1(last, chain)
            split(L2, 1, chain)
            tail1_norm(last, chain)
            for k in range(2, GROUPS):
                split(L2, k, chain)
            looped(tail2)
            self_term(last)
            split(L3, 0, chain)
            split(L3, 1, chain)
            tail2_norm(last, chain)
            split(L3, 2, chain)
            tail2a(last, chain)
            split(L3, 3, chain)
            tail2b(last, chain)
            split(L3, 4, chain)
            tail2c(last, chain)
            for k in range(5, GROUPS):
                split(L3, k, chain)
            looped(tail3)
            tail3(GROUPS - 1, chain)


_INS = ['x', 'adj', 'L0_gnn_W_msg', 'L0_gnn_b_msg', 'L0_gnn_W_ih', 'L0_gnn_W_hh', 'L0_gnn_b_ih', 'L0_gnn_b_hh',
        'L1_gnn_weight', 'L1_gnn_att_src', 'L1_gnn_att_dst', 'L2_gnn_weight', 'L3_gnn_W']
_OUTS = [((4096, 128), 'float32')]


def kernel(**inputs):
    import numpy as _np
    import concourse.bacc as _bacc
    from concourse import mybir as _mybir
    from concourse.bass_utils import run_bass_kernel_spmd as _run

    nc = _bacc.Bacc("TRN2", target_bir_lowering=False, num_devices=1)
    arrays, args = {}, []
    for name in _INS:
        a = _np.ascontiguousarray(inputs[name])
        arrays[f"in_{name}_dram"] = a
        args.append(nc.dram_tensor(f"in_{name}_dram", a.shape, _mybir.dt.from_np(a.dtype), kind="ExternalInput").ap())
    for i, (shape, dtype) in enumerate(_OUTS):
        dt = _mybir.dt.from_np(_np.dtype(dtype))
        args.append(nc.dram_tensor(f"out_{i}_dram", shape, dt, kind="ExternalOutput").ap())
    adjacency_stack(nc, *args)
    r = _run(nc, [arrays], core_ids=[0])
    return r.results[0]["out_0_dram"]
```

```python
import math

import numpy as np
import concourse.bass as bass
from concourse import mybir
from contextlib import ExitStack

F32 = mybir.dt.float32
F32R = mybir.dt.float32r
ALU = mybir.AluOpType
ACT = mybir.ActivationFunctionType
AX = mybir.AxisListType


def adjacency_stack(nc, x, adj, w_msg, b_msg, w_ih, w_hh, b_ih, b_hh, w_att, att_src, att_dst, w_gcn, w_hyp, out):
    P = 128
    N, D = x.shape
    BLOCKS = N // P
    B = 4
    C = B * P
    GROUPS = N // C
    SLOTS = 4
    TILES = N // C
    LAG = 4
    LN_EPS, EPS, MIN_NORM, CLAMP, DEG_EPS = 1e-5, 1e-5, 1e-15, 1e-10, 1e-8
    TOP = float(np.float32(1.0 - EPS))
    ATANH_MAX = 0.5 * math.log((1.0 + TOP) / (1.0 - TOP))
    WBUFS, PBUFS = 16, 8
    L0, L1, L2, L3 = range(4)
    AGG = {L0: 0, L2: 1, L3: 2}

    ctx = ExitStack()
    with ctx:
        def sb(name, shape, dt=F32):
            return ctx.enter_context(nc.sbuf_tensor(name, shape, dt))

        def pb(name):
            return ctx.enter_context(nc.psum_tensor(name, [P, C], F32))

        def sem(name):
            return ctx.enter_context(nc.semaphore(name))

        x_all = sb("x_all", [P, BLOCKS, D])
        with nc.sbuf_tensor("att_p", [P, PBUFS, C], F32) as att_p:
            pass
        src_hi = sb("src_hi", [P, BLOCKS, D], F32R)
        with nc.sbuf_tensor("att_w", [P, WBUFS, C], F32) as att_w:
            pass
        src_lo = sb("src_lo", [P, BLOCKS, D], F32R)
        t_hi = sb("t_hi", [P, LAG, C], F32R)
        t_lo = sb("t_lo", [P, LAG, C], F32R)
        nat_a = sb("nat_a", [P, BLOCKS, D])
        nat_b = sb("nat_b", [P, BLOCKS, D])
        with nc.sbuf_tensor("dst_row", [P, N], F32) as dst_row:
            pass
        q_pair = sb("q_pair", [P, BLOCKS, P], F32R)
        exp_s = sb("exp_s", [P, BLOCKS])
        exp_ms = sb("exp_ms", [P, BLOCKS])
        deg_part = sb("deg_part", [P, BLOCKS, GROUPS])
        rowsum = sb("rowsum", [P, BLOCKS])
        dinv = sb("dinv", [P, BLOCKS])
        q_all = sb("q_all", [P, BLOCKS])

        ring = sb("ring", [P, SLOTS, B, C])
        junk = sb("junk", [P, 2, C], mybir.dt.bfloat16)

        agg_t = sb("agg_t", [P, C])
        msg_t = sb("msg_t", [P, C])
        r_t = sb("r_t", [P, C])
        z_t = sb("z_t", [P, C])
        n_t = sb("n_t", [P, C])
        pre_t = sb("pre_t", [P, C])
        x_new = sb("x_new", [P, B, D])
        h_new = sb("h_new", [P, B, D])
        h_t = sb("h_t", [P, C])
        y_nat = sb("y_nat", [P, B, D])
        tmp = sb("tmp", [P, B, D])
        den_s = sb("den_s", [P, C])
        st6 = sb("st6", [P, B, 6])
        mv = sb("mv", [P, B, 2])
        rstd = sb("rstd", [P, B])
        nbias = sb("nbias", [P, B])
        rden = sb("rden", [P, B])
        den2_acc = sb("den2_acc", [P, 2, C])
        den2_s = sb("den2_s", [P, C])
        NSC = 24
        sc = sb("sc", [P, NSC, B])
        SC = {n: sc[:, i, :] for i, n in enumerate(
            ["xn2", "xn", "ss", "mxn", "arg", "ln", "z2", "ser", "mask", "ath", "z", "t", "f", "g", "den",
             "sgn", "c", "un", "k", "one", "inv", "xc", "rec"])}

        ident = sb("ident", [P, P])
        avg32 = sb("avg32", [P, 1])
        ones = sb("ones", [P, 1])
        avg64 = sb("avg64", [P, 1])
        mhalf = sb("mhalf", [P, BLOCKS])
        phalf = sb("phalf", [P, B])
        ln_eps = sb("ln_eps", [P, B])
        minus_one = sb("minus_one", [P, B])
        w_nat = sb("w_nat", [P, 8, D])
        w_t = sb("w_t", [P, 8, D])
        w_gcn_s = sb("w_gcn_s", [P, D])
        w_hyp_s = sb("w_hyp_s", [P, D])
        att_cols = sb("att_cols", [P, 2])
        w_src = sb("w_src", [P, 1])
        w_dst = sb("w_dst", [P, P])
        bias = sb("bias", [P, 7])
        bias_g = sb("bias_g", [P, 2])

        t_ps = [pb(f"t_ps{i}") for i in range(LAG)]
        acc_ps = pb("acc_ps")
        e0, e1, e2 = pb("e0"), pb("e1"), pb("e2")
        den_ps = t_ps[3]
        den3_ps = e2

        def vector_den(jb):
            return jb >= 5 and jb % 4 != 0

        GRU_AT = {
            "hidden": (LAG, 0), "acc": (LAG - 2, 0), "msg": (5, 1), "relu": (6, 5), "rz": (8, 3), "hn": (9, 4),
            "r_tanh": (9, 8), "z_tanh": (10, 9), "r": (10, 10), "rh": (11, 11), "in": (11, 6),
            "npre": (12, 13), "n": (14, 14), "mix": (15, 15), "mixed": (16, 16), "to_nodes": (19, 16), "x_new": (20, 19),
            "keep_x": (21, 20), "stats": (21, 19), "norm": (24, 21), "hT": (27, 20), "h_t": (28, 24), "proj": (30, 23),
            "exps": (31, 26), "att_src": (31, 28)}

        WEIGHTS_AT = 12
        H0_AT = [WEIGHTS_AT + 3 + 2 * k for k in range(GROUPS)]

        def due(step, e, jb):
            return jb == GRU_AT[step][isinstance(e, int)]

        def nodes(ps):
            return ps[:, :].rearrange("p (b d) -> p b d", b=B)

        def grp(t, g):
            return t[:, bass.ds(g * B, B), :]

        def cols(t, g):
            return t[:, bass.ds(g * B, B)]

        def wide(col):
            return col.rearrange("p (b o) -> p b o", o=1).to_broadcast([P, B, D])

        x_in = [sem(f"x_in{i}") for i in range(GROUPS // 2 + 1)]
        w_in = sem("w_in")
        adj_in = [sem(f"adj_in{i}") for i in range(SLOTS)]
        row_summed, last_summed = sem("row_summed"), sem("last_summed")
        t_ready, hi_ready, lo_ready = sem("t_ready"), sem("hi_ready"), sem("lo_ready")
        w_made, p_made, att_mm = sem("w_made"), sem("p_made"), sem("att_mm")
        den_mm, q_ready = sem("den_mm"), sem("q_ready")
        den3_free, den2_kept = sem("den3_free"), sem("den2_kept")
        acc_done, acc_free, den_free = sem("acc_done"), sem("acc_free"), sem("den_free")
        const_step, const_ready = sem("const_step"), sem("const_ready")
        wt_ps, wt_ready, wv_ps, wv_ready, bias_ready = (sem(n) for n in ("wt_ps", "wt_ready", "wv_ps", "wv_ready", "bias_ready"))
        ln_stats, ln_mv, ln_rstd, ln_scaled, ln_done = (sem(n) for n in ("ln_stats", "ln_mv", "ln_rstd", "ln_scaled", "ln_done"))
        src_ready, hi_split = sem("src_ready"), sem("hi_split")
        h0_ps, h0_t = sem("h0_ps"), sem("h0_t")
        x_kept, xnew_ready = sem("x_kept"), sem("xnew_ready")
        gh_ps, msg_ps, msg_ready, rz_ps, hn_ps, in_ps = (sem(n) for n in ("gh_ps", "msg_ps", "msg_ready", "rz_ps", "hn_ps", "in_ps"))
        r_tanh, z_tanh, r_ready, z_ready, rh_ready, npre_ready, n_ready = (sem(n) for n in (
            "r_tanh", "z_tanh", "r_ready", "z_ready", "rh_ready", "npre_ready", "n_ready"))
        mix_step, gru_out, gru_nat = sem("mix_step"), sem("gru_out"), sem("gru_nat")
        hT_ps, hT_ready = sem("hT_ps"), sem("hT_ready")
        proj_ps, exps_ready, att_src_ready = sem("proj_ps"), sem("exps_ready"), sem("att_src_ready")
        den_ps_ready, rden_ready, z_norm, z_nat, num_copied = (sem(n) for n in ("den_ps_ready", "rden_ready", "z_norm", "z_nat", "num_copied"))
        deg_done, dinv_step, dinv_ready, rowsum_ready = sem("deg_done"), sem("dinv_step"), sem("dinv_ready"), sem("rowsum_ready")
        self_ready, self_ps, self_t = sem("self_ready"), sem("self_ps"), sem("self_t")
        gcn_ps, gcn_scaled = sem("gcn_ps"), sem("gcn_scaled")
        mx_ps, mx_ready = sem("mx_ps"), sem("mx_ready")
        pool_step = sem("pool_step")
        ln_arg, ln_val, th_arg, th_val = sem("ln_arg"), sem("ln_val"), sem("th_arg"), sem("th_val")
        v_nat, v_ready, den_nat, den_ready = sem("v_nat"), sem("v_ready"), sem("den_nat"), sem("den_ready")
        ln_arg3, ln_val3, th_arg3, th_val3 = sem("ln_arg3"), sem("ln_val3"), sem("th_arg3"), sem("th_val3")
        c_ready, k_ready = sem("c_ready"), sem("k_ready")
        out_ready, out_stored = sem("out_ready"), sem("out_stored")
        hyp_src_ready = sem("hyp_src_ready")
        scaled_src = sem("scaled_src")
        xn2_ready, u_made, un2_ready = sem("xn2_ready"), sem("u_made"), sem("un2_ready")

        block = ctx.enter_context(nc.Block())

        def passes(engine, body, apart=False):
            for p in (L0, L1, L2, L3):
                body(p, 0, True)
                last = GROUPS - (apart and p == L1)
                with engine.Fori(1, last) as g:
                    body(p, g, False)
                if last < GROUPS:
                    body(p, last, False)

        @block.sync
        def _(sp):
            def load_x(b):
                sp.dma_start(grp(x_all, b), x[b * C:(b + 1) * C, :].rearrange("(b p) d -> p b d", p=P)).then_inc(x_in[(b + 1) // 2], 16)

            def body(p, g, first):
                for k in range(TILES):
                    s, wrap = k % SLOTS, k < SLOTS
                    q = p - 1 if first and wrap else p
                    done = (TILES * GROUPS if first and wrap else TILES * g) + k - SLOTS + 1
                    if q == L0:
                        sp.wait_ge(hi_ready, done * B)
                    elif q in AGG:
                        sp.wait_ge(t_ready, (AGG[q] * TILES * GROUPS + done) * B)
                    elif q == L1:
                        sp.wait_ge(p_made, done * B)
                        if p == L1 and not (isinstance(g, int) and g == GROUPS - 1 and not wrap):
                            sp.wait_ge(row_summed, done * B)
                    row, col = (k, g) if p == L1 else (g, k)
                    tile = adj[bass.ds(row * C, C), bass.ds(col * C, C)]
                    sp.dma_start(ring[:, s, :, :], tile.rearrange("(b p) c -> p b c", p=P)).then_inc(adj_in[s], 16)
                    if p == L0 and first and k < GROUPS // 2:
                        for b in range(2 * k + 1, min(2 * k + 3, GROUPS)):
                            load_x(b)

            sp.sem_inc(out_stored, 16)
            load_x(0)
            passes(sp, body, apart=True)
            sp.wait_ge(out_stored, 16 * (GROUPS + 1))

        def tile_arrived(engine, p, g, k):
            engine.wait_ge(adj_in[k % SLOTS], 16 * ((p * GROUPS + g) * (TILES // SLOTS) + k // SLOTS + 1))

        @block.tensor
        def _(pe):
            def weights():
                pe.wait_ge(w_in, 16 * 11)
                for i in range(8):
                    last = nc.tensor.transpose((e0 if i < 4 else e1)[:, bass.ds((i % 4) * P, P)], w_nat[:, i, :], ident[:, :])
                last.then_inc(wt_ps, 1)
                nc.tensor.matmul(e2[:, 0:1], w_nat[:, 7, :], att_cols[:, 0:1], start=True, stop=True)
                nc.tensor.matmul(e2[:, P:2 * P], w_nat[:, 7, :], att_cols[:, 1:2].to_broadcast([P, P]),
                                 start=True, stop=True).then_inc(wv_ps, 1)

            def transpose4(dst, src):
                for b in range(B):
                    last = nc.tensor.transpose(dst[:, b * P:(b + 1) * P], src(b), ident[:, :])
                return last

            def hT(c):
                pe.wait_ge(ln_done, c + 1)
                transpose4(e1, lambda b: h_new[:, b, :]).then_inc(hT_ps, 1)

            def tail0(e, jb):
                if due("hidden", e, jb):
                    pe.wait_ge(h0_t, GROUPS)
                    hid = nat_b_t(e)
                    nc.tensor.matmul(e0[:, :], w_t[:, 4, :], hid, start=True, stop=False)
                    nc.tensor.matmul(e1[:, :], w_t[:, 5, :], hid, start=True, stop=False)
                if due("msg", e, jb):
                    pe.wait_ge(acc_free, e + 1)
                    nc.tensor.matmul(e2[:, :], w_t[:, 0, :], agg_t[:, :], start=True, stop=True).then_inc(msg_ps, 1)
                if due("rz", e, jb):
                    pe.wait_ge(msg_ready, e + 1)
                    nc.tensor.matmul(e0[:, :], w_t[:, 1, :], msg_t[:, :], start=False, stop=True).then_inc(rz_ps, 1)
                    nc.tensor.matmul(e1[:, :], w_t[:, 2, :], msg_t[:, :], start=False, stop=True).then_inc(rz_ps, 1)
                if due("hn", e, jb):
                    nc.tensor.matmul(e2[:, :], w_t[:, 6, :], nat_b_t(e), start=True, stop=True).then_inc(hn_ps, 1)
                if due("in", e, jb):
                    pe.wait_ge(r_tanh, e + 1)
                    nc.tensor.matmul(e0[:, :], w_t[:, 3, :], msg_t[:, :], start=True, stop=True).then_inc(in_ps, 1)
                if due("to_nodes", e, jb):
                    pe.wait_ge(gru_out, e + 1)
                    pe.wait_ge(z_tanh, e + 1)
                    transpose4(e1, lambda b: n_t[:, b * P:(b + 1) * P]).then_inc(gru_nat, 1)
                if due("hT", e, jb):
                    hT(GROUPS + e)
                if due("proj", e, jb):
                    pe.wait_ge(hT_ready, e + 1)
                    pe.wait_ge(npre_ready, e + 1)
                    for b in range(B):
                        nc.tensor.matmul(e0[:, b * P:(b + 1) * P], h_t[:, b * P:(b + 1) * P], w_t[:, 7, :], start=True, stop=True)
                    nc.tensor.matmul(e1[:, :], w_dst[:, :], h_t[:, :], start=True, stop=True)
                    for b in range(B):
                        last = nc.tensor.matmul(e2[:, b:b + 1], h_t[:, b * P:(b + 1) * P], w_src[:, :], start=True, stop=True)
                    last.then_inc(proj_ps, 1)

            def nat_b_t(e):
                return nat_b[:, bass.ds(e * B, B), :].rearrange("p b d -> p (b d)")

            def tail1(e, jb):
                if jb == (3 if isinstance(e, int) else 2):
                    pe.wait_ge(acc_free, GROUPS + e + 1)
                    pe.wait_ge(den_free, e + 1)
                    for b in range(B):
                        last = nc.tensor.matmul(e0[:, b:b + 1], den_s[:, b * P:(b + 1) * P], avg32[:, :], start=True, stop=True)
                    last.then_inc(den_ps_ready, 1)
                    transpose4(e1, lambda b: agg_t[:, b * P:(b + 1) * P]).then_inc(z_nat, 1)

            def tail2(e, jb):
                if jb == 5:
                    pe.wait_ge(acc_free, 2 * GROUPS + e + 1)
                    for b in range(B):
                        last = nc.tensor.matmul(e0[:, b * P:(b + 1) * P], agg_t[:, b * P:(b + 1) * P], w_gcn_s[:, :], start=True, stop=True)
                    last.then_inc(gcn_ps, 1)
                if jb == 14:
                    hT(3 * GROUPS + e)
                if jb == 17:
                    pe.wait_ge(hT_ready, GROUPS + e + 1)
                    for b in range(B):
                        last = nc.tensor.matmul(e0[:, b * P:(b + 1) * P], h_t[:, b * P:(b + 1) * P], w_hyp_s[:, :], start=True, stop=True)
                    last.then_inc(mx_ps, 1)

            def tail3(e, jb):
                if jb == 6:
                    pe.wait_ge(acc_free, 3 * GROUPS + e + 1)
                    pe.wait_ge(den3_free, e + 1)
                    pe.wait_ge(den2_kept, e + 1)
                    transpose4(e0, lambda b: agg_t[:, b * P:(b + 1) * P]).then_inc(v_nat, 1)
                    for b in range(B):
                        nc.tensor.matmul(e1[:, b:b + 1], den_s[:, b * P:(b + 1) * P], avg64[:, :], start=True, stop=False)
                        last = nc.tensor.matmul(e1[:, b:b + 1], den2_s[:, b * P:(b + 1) * P], ones[:, :], start=False, stop=True)
                    last.then_inc(den_nat, 1)

            TAILS = {L0: tail0, L1: tail1, L2: tail2, L3: tail3}

            def products(p, g, jb):
                unit = (AGG[p] * GROUPS + g) * BLOCKS + jb
                pe.wait_ge(lo_ready, unit + 1)
                if jb == 0 and not (p == L0 and isinstance(g, int)):
                    pe.wait_ge(acc_free, p * GROUPS + g)
                if jb % B == 0 and (jb == BLOCKS - LAG or isinstance(g, int) and g == 0):
                    pe.wait_ge(src_ready, AGG[p] * GROUPS + jb // B + 1)
                b = jb % LAG
                first, last = jb == 0, jb == BLOCKS - 1
                nc.tensor.matmul(acc_ps[:, :], src_hi[:, jb, :], t_hi[:, b, :], start=first, stop=False)
                nc.tensor.matmul(acc_ps[:, :], src_lo[:, jb, :], t_hi[:, b, :], start=False, stop=False)
                if p == L3 and jb == 0 and not isinstance(g, int):
                    pe.wait_ge(den3_free, g)
                if p == L3 and not vector_den(jb):
                    nc.tensor.matmul(den3_ps[:, :], q_pair[:, jb, :], t_hi[:, b, :], start=first, stop=False)
                    nc.tensor.matmul(den3_ps[:, :], q_pair[:, jb, :], t_lo[:, b, :], start=False, stop=jb == BLOCKS - B)
                mm = nc.tensor.matmul(acc_ps[:, :], src_hi[:, jb, :], t_lo[:, b, :], start=False, stop=last)
                if last:
                    mm.then_inc(acc_done, 1)

            def body(p, g, first):
                if p == L1:
                    for jb in range(BLOCKS):
                        if first:
                            tail0(GROUPS - 1, jb)
                        else:
                            tail1(g - 1, jb)
                        if jb == 0:
                            pe.wait_ge(acc_free, GROUPS + g)
                        if first and jb % B == 0:
                            pe.wait_ge(att_src_ready, jb // B + 1)
                        if jb % 2 == 0:
                            pe.wait_ge(p_made, g * BLOCKS + jb + 2)
                        nc.tensor.matmul(acc_ps[:, :], nat_a[:, jb, :], att_p[:, jb % PBUFS, :], start=jb == 0,
                                         stop=jb == BLOCKS - 1).then_inc(att_mm, 1)
                        if jb == B - 1 and not first:
                            pe.wait_ge(den_free, g)
                        if jb % B == B - 1:
                            for q in range(B):
                                j = jb - B + 1 + q
                                last = nc.tensor.matmul(den_ps[32 * q:32 * q + 32, :], exp_s[:, j:j + 1].to_broadcast([P, 32]),
                                                        att_w[:, j % WBUFS, :], start=jb == B - 1, stop=jb == BLOCKS - 1)
                            last.then_inc(den_mm, 1)
                    return
                for jb in range(BLOCKS):
                    if first:
                        if p == L0:
                            if jb == WEIGHTS_AT:
                                weights()
                            if jb in H0_AT:
                                k = H0_AT.index(jb)
                                pe.wait_ge(ln_done, k + 1)
                                if k > 1:
                                    pe.wait_ge(h0_t, k - 1)
                                elif k == 0:
                                    pe.wait_ge(wt_ready, 2)
                                transpose4((e0, e1)[k % 2], lambda b: nat_a[:, k * B + b, :]).then_inc(h0_ps, 1)
                        elif p == L2:
                            tail1(GROUPS - 1, jb)
                        else:
                            tail2(GROUPS - 1, jb)
                    else:
                        TAILS[p](g - 1, jb)
                    if p == L2 and jb == (20 if first else LAG):
                        pe.wait_ge(self_ready, g + 1)
                        transpose4(e1, lambda b: tmp[:, b, :]).then_inc(self_ps, 1)
                    if jb >= LAG:
                        products(p, g, jb - LAG)
                    elif not first:
                        products(p, g - 1, BLOCKS - LAG + jb)
                    elif p == L3:
                        products(L2, GROUPS - 1, BLOCKS - LAG + jb)
                    if jb % B == 0:
                        tile_arrived(pe, p, g, jb // B)
                    if p == L2 and first and jb == 3:
                        pe.wait_ge(den_free, GROUPS)
                    for b in range(B):
                        last = nc.tensor.transpose(t_ps[jb % LAG][:, b * P:(b + 1) * P],
                                                   ring[:, (jb // B) % SLOTS, b, (jb % B) * P:(jb % B + 1) * P], ident[:, :])
                    last.then_inc(t_ready, 1)

            def flush(p):
                for jb in range(BLOCKS - LAG, BLOCKS):
                    products(p, GROUPS - 1, jb)

            pe.wait_ge(const_ready, 1)
            for p in (L0, L1, L2, L3):
                body(p, 0, True)
                with pe.Fori(1, GROUPS) as g:
                    body(p, g, False)
                if p in (L0, L3):
                    flush(p)
            for jb in range(BLOCKS):
                tail3(GROUPS - 1, jb)

        @block.scalar
        def _(act):
            def load(dst, src):
                act.dma_start(dst, src).then_inc(w_in, 16)

            load(w_nat[:, 0, :], w_msg)
            load(w_nat[:, 1:4, :], w_ih.rearrange("(t p) d -> p t d", p=P))
            load(w_nat[:, 4:7, :], w_hh.rearrange("(t p) d -> p t d", p=P))
            load(w_nat[:, 7, :], w_att)

            def weights():
                act.wait_ge(wt_ps, 1)
                nc.scalar.activation(w_t[:, 0:4, :], nodes(e0), ACT.Copy).then_inc(wt_ready, 1)
                nc.scalar.activation(w_t[:, 4:8, :], nodes(e1), ACT.Copy).then_inc(wt_ready, 1)
                act.wait_ge(wv_ps, 1)
                nc.scalar.activation(w_src[:, :], e2[:, 0:1], ACT.Copy).then_inc(wv_ready, 1)
                nc.scalar.activation(w_dst[:, :], e2[:, P:2 * P], ACT.Copy).then_inc(wv_ready, 1)

            def hT(c):
                act.wait_ge(hT_ps, c + 1)
                nc.scalar.activation(h_t[:, :], e1[:, :], ACT.Copy).then_inc(hT_ready, 1)

            def tail0(e, jb):
                if due("relu", e, jb):
                    act.wait_ge(msg_ps, e + 1)
                    nc.scalar.activation(msg_t[:, :], e2[:, :], ACT.Relu, bias=bias[:, 0:1]).then_inc(msg_ready, 1)
                if due("r_tanh", e, jb):
                    act.wait_ge(rz_ps, 2 * e + 1)
                    nc.scalar.activation(r_t[:, :], e0[:, :], ACT.Tanh, bias=bias_g[:, 0:1], scale=0.5).then_inc(r_tanh, 1)
                if due("z_tanh", e, jb):
                    act.wait_ge(rz_ps, 2 * e + 2)
                    nc.scalar.activation(z_t[:, :], e1[:, :], ACT.Tanh, bias=bias_g[:, 1:2], scale=0.5).then_inc(z_tanh, 1)
                if due("n", e, jb):
                    act.wait_ge(npre_ready, e + 1)
                    nc.scalar.activation(n_t[:, :], pre_t[:, :], ACT.Tanh, bias=bias[:, 3:4]).then_inc(n_ready, 1)
                if due("keep_x", e, jb):
                    keep_x(L0, e)
                if due("h_t", e, jb):
                    hT(e)
                if due("exps", e, jb):
                    act.wait_ge(proj_ps, e + 1)
                    nc.scalar.activation(cols(exp_s, e), e2[:, 0:B], ACT.Exp).then_inc(exps_ready, 1)
                    nc.scalar.activation(cols(exp_ms, e), e2[:, 0:B], ACT.Exp, scale=-0.8).then_inc(exps_ready, 1)
                    nc.scalar.activation(dst_row[:, bass.ds(e * C, C)], e1[:, :], ACT.Exp, scale=0.8).then_inc(exps_ready, 1)

            def tail1(e, jb):
                if jb == 0:
                    act.wait_ge(att_mm, (e + 1) * BLOCKS)
                    nc.scalar.activation(agg_t[:, :], acc_ps[:, :], ACT.Copy).then_inc(acc_free, 1)
                    act.wait_ge(den_mm, (e + 1) * (BLOCKS // B))
                    nc.scalar.activation(den_s[:, :], den_ps[:, :], ACT.Copy).then_inc(den_free, 1)
                if jb == 8:
                    keep_x(L1, e)
                if jb == 10:
                    act.wait_ge(ln_rstd, 2 * GROUPS + e + 1)
                    for b in range(B):
                        last = nc.scalar.activation(nat_b[:, bass.ds(e * B + b, 1), :], x_new[:, b:b + 1, :], ACT.Relu,
                                                    bias=nbias[:, b:b + 1], scale=rstd[:, b:b + 1])
                    last.then_inc(ln_done, 1)

            def keep_x(layer, e):
                act.wait_ge(xnew_ready, layer * GROUPS + e + 1)
                nc.scalar.activation(grp(x_all, e), x_new[:, :, :], ACT.Copy).then_inc(x_kept, 1)

            def squares(dst, src):
                for b in range(B):
                    last = nc.scalar.activation(junk[:, 0, b * D:(b + 1) * D], src[:, b, :], ACT.Square, accum_out=SC[dst][:, b:b + 1])
                return last

            def tail2(e, jb):
                if jb == 10:
                    keep_x(L2, e)
                if jb == 13:
                    act.wait_ge(ln_done, 3 * GROUPS + e + 1)
                    squares("xn2", h_new).then_inc(xn2_ready, 1)
                if jb == 15:
                    hT(GROUPS + e)
                if jb == 18:
                    act.wait_ge(mx_ps, e + 1)
                    nc.scalar.activation(y_nat[:, :, :], nodes(e0), ACT.Copy)
                    squares("ss", nodes(e0)).then_inc(mx_ready, 1)
                if jb == 17:
                    act.wait_ge(ln_arg, e + 1)
                    nc.scalar.activation(SC["ln"], SC["arg"], ACT.Ln).then_inc(ln_val, 1)
                if jb == 22:
                    act.wait_ge(th_arg, e + 1)
                    nc.scalar.activation(SC["t"], SC["z"], ACT.Tanh).then_inc(th_val, 1)

            def tail3(e, jb):
                if jb == LAG - 2:
                    act.wait_ge(acc_done, 2 * GROUPS + e + 1)
                    nc.scalar.activation(den_s[:, :], den3_ps[:, :], ACT.Copy).then_inc(den3_free, 1)
                if jb == 7:
                    act.wait_ge(v_nat, e + 1)
                    nc.scalar.activation(y_nat[:, :, :], nodes(e0), ACT.Copy)
                    squares("ss", nodes(e0)).then_inc(v_ready, 1)
                if jb == 15:
                    act.wait_ge(ln_arg3, e + 1)
                    nc.scalar.activation(SC["ln"], SC["arg"], ACT.Ln).then_inc(ln_val3, 1)
                if jb == 22:
                    act.wait_ge(u_made, e + 1)
                    squares("ss", h_new).then_inc(un2_ready, 1)
                if jb == 25:
                    act.wait_ge(th_arg3, e + 1)
                    nc.scalar.activation(SC["t"], SC["un"], ACT.Tanh).then_inc(th_val3, 1)
                if jb == BLOCKS - 1:
                    act.wait_ge(out_ready, e + 1)
                    act.dma_start(out[bass.ds(e * C, C), :].rearrange("(b p) d -> p b d", p=P), x_new[:, :, :]).then_inc(out_stored, 16)

            TAILS = {L0: tail0, L1: tail1, L2: tail2, L3: tail3}

            def source_hi(p, k):
                blk = slice(k * B, (k + 1) * B)
                if p == L0:
                    act.wait_ge(ln_done, k + 1)
                elif p == L2:
                    act.wait_ge(scaled_src, k + 1)
                    act.wait_ge(att_mm, GROUPS * BLOCKS - PBUFS + k + 1)
                else:
                    act.wait_ge(hyp_src_ready, k + 1)
                    act.wait_ge(t_ready, (AGG[L2] * GROUPS + GROUPS - 1) * BLOCKS + (k + 1) * B + LAG)
                nc.scalar.activation(src_hi[:, blk, :], (nat_b if p == L2 else nat_a)[:, blk, :], ACT.Copy).then_inc(hi_split, 1)

            def body(p, g, first):
                for jb in range(BLOCKS):
                    if first and p:
                        TAILS[p - 1](GROUPS - 1, jb)
                    elif not first:
                        TAILS[p](g - 1, jb)
                    if p == L2 and jb == (19 if first else 2):
                        if first:
                            act.wait_ge(scaled_src, 1)
                        nc.scalar.activation(tmp[:, :, :], grp(nat_b, g), ACT.Copy).then_inc(self_ready, 1)
                    if p == L2 and jb == (21 if first else 5):
                        if not first:
                            act.wait_ge(acc_free, 2 * GROUPS + g)
                        act.wait_ge(self_ps, g + 1)
                        nc.scalar.activation(pre_t[:, :], e1[:, :], ACT.Copy).then_inc(self_t, 1)
                    if p == L1 and not (isinstance(g, int) and g == GROUPS - 1):
                        if jb % B == 0:
                            tile_arrived(act, p, g, jb // B)
                        if first and jb < 2:
                            act.wait_ge(last_summed, GROUPS * B + jb - 1)
                        else:
                            act.wait_ge(row_summed, g * BLOCKS + jb - 1)
                        nc.scalar.activation(junk[:, jb % 2, :], ring[:, (jb // B) % SLOTS, jb % B, :], ACT.Copy,
                                             accum_out=deg_part[:, jb, bass.ds(g, 1)]).then_inc(row_summed, 1)
                    if p == L0 and jb // B == TILES - 1:
                        if jb % B == 0:
                            tile_arrived(act, p, g, TILES - 1)
                        if not (first and jb % B < 2):
                            act.wait_ge(last_summed, g * B + jb % B - 1)
                        nc.scalar.activation(junk[:, jb % 2, :], ring[:, (TILES - 1) % SLOTS, jb % B, :], ACT.Copy,
                                             accum_out=deg_part[:, bass.ds(g * B + jb % B, 1), TILES - 1]).then_inc(last_summed, 1)
                    if p == L1:
                        continue
                    if p == L0 and first and jb % B == 1 and jb // B + 1 < GROUPS:
                        source_hi(p, jb // B + 1)
                    if first and p in (L2, L3) and (jb % 2 == 0 and jb // 2 < GROUPS - 1 or jb == (15 if p == L2 else 28)):
                        source_hi(p, min(jb // 2, GROUPS - 1))
                    act.wait_ge(t_ready, (AGG[p] * GROUPS + g) * BLOCKS + jb + 1)
                    nc.scalar.activation(t_hi[:, jb % LAG, :], t_ps[jb % LAG][:, :], ACT.Copy).then_inc(hi_ready, 1)
                    if p == L0 and first and jb == WEIGHTS_AT + 1:
                        weights()
                    if p == L0 and first and jb in H0_AT:
                        k = H0_AT.index(jb)
                        act.wait_ge(h0_ps, k + 1)
                        nc.scalar.activation(nat_b[:, k * B:(k + 1) * B, :], nodes((e0, e1)[k % 2]), ACT.Copy).then_inc(h0_t, 1)

            source_hi(L0, 0)
            load(w_gcn_s[:, :], w_gcn)
            load(w_hyp_s[:, :], w_hyp)
            with nc.allow_non_contiguous_dma(reason="a few hundred floats, one per partition"):
                load(att_cols[:, 0:1], att_src.rearrange("o d -> d o"))
                load(att_cols[:, 1:2], att_dst.rearrange("o d -> d o"))
                load(bias[:, 0:1], b_msg.rearrange("(o d) -> d o", o=1))
                load(bias[:, 1:4], b_ih.rearrange("(t d) -> d t", t=3))
                load(bias[:, 4:7], b_hh.rearrange("(t d) -> d t", t=3))
            passes(act, body, apart=True)
            for jb in range(BLOCKS):
                tail3(GROUPS - 1, jb)

        @block.vector
        def _(dve):
            def stats(c, src):
                for b in range(B):
                    last = nc.vector.bn_stats(st6[:, b, :], src(b))
                dve.drain()
                for b in range(B):
                    last = nc.vector.bn_aggr(mv[:, b, :], st6[:, b, :])
                last.then_inc(ln_mv, 1)

            def normalise(c, src, dst, n):
                dve.wait_ge(ln_rstd, c + 1)
                for b in range(B):
                    last = nc.vector.tensor_scalar(h_new[:, b, :], src(b), mv[:, b, 0:1], rstd[:, b:b + 1], ALU.subtract, ALU.mult)
                last.then_inc(ln_scaled, 1)
                dve.wait_ge(ln_scaled, n + 1)
                nc.vector.tensor_scalar(dst, h_new[:, :, :], 0.0, None, ALU.max).then_inc(ln_done, 1)

            def tail0(e, jb):
                if due("acc", e, jb):
                    dve.wait_ge(acc_done, e + 1)
                    nc.vector.tensor_copy(agg_t[:, :], acc_ps[:, :]).then_inc(acc_free, 1)
                if due("r", e, jb):
                    dve.wait_ge(r_tanh, e + 1)
                    nc.vector.tensor_scalar(r_t[:, :], r_t[:, :], 0.5, 0.5, ALU.mult, ALU.add).then_inc(r_ready, 1)
                if due("rh", e, jb):
                    dve.wait_ge(r_ready, e + 1)
                    dve.wait_ge(hn_ps, e + 1)
                    nc.vector.scalar_tensor_tensor(pre_t[:, :], e2[:, :], bias[:, 6:7], r_t[:, :], ALU.add, ALU.mult).then_inc(rh_ready, 1)
                if due("npre", e, jb):
                    dve.wait_ge(rh_ready, e + 1)
                    dve.wait_ge(in_ps, e + 1)
                    nc.vector.tensor_tensor(pre_t[:, :], e0[:, :], pre_t[:, :], ALU.add).then_inc(npre_ready, 1)
                if due("mix", e, jb):
                    dve.wait_ge(n_ready, e + 1)
                    hid = nat_b[:, bass.ds(e * B, B), :].rearrange("p b d -> p (b d)")
                    nc.vector.tensor_tensor(msg_t[:, :], hid, n_t[:, :], ALU.subtract).then_inc(mix_step, 1)
                    dve.wait_ge(mix_step, 2 * e + 1)
                    nc.vector.scalar_tensor_tensor(msg_t[:, :], z_t[:, :], 1.0, msg_t[:, :], ALU.add, ALU.mult).then_inc(mix_step, 1)
                if due("mixed", e, jb):
                    dve.wait_ge(mix_step, 2 * e + 2)
                    nc.vector.scalar_tensor_tensor(n_t[:, :], msg_t[:, :], 0.5, n_t[:, :], ALU.mult, ALU.add).then_inc(gru_out, 1)
                if due("x_new", e, jb):
                    dve.wait_ge(gru_nat, e + 1)
                    nc.vector.tensor_tensor(x_new[:, :, :], nodes(e1), grp(x_all, e), ALU.add).then_inc(xnew_ready, 1)
                if due("stats", e, jb):
                    dve.wait_ge(xnew_ready, e + 1)
                    stats(GROUPS + e, lambda b: x_new[:, b, :])
                if due("norm", e, jb):
                    normalise(GROUPS + e, lambda b: x_new[:, b, :], h_new[:, :, :], GROUPS + e)
                if due("att_src", e, jb):
                    dve.wait_ge(exps_ready, 3 * e + 1)
                    nc.vector.tensor_tensor(grp(nat_a, e), nodes(e0), wide(cols(exp_s, e)), ALU.mult).then_inc(att_src_ready, 1)

            def tail1(e, jb):
                if jb == 6:
                    dve.wait_ge(den_ps_ready, e + 1)
                    nc.vector.reciprocal(rden[:, :], e0[:, 0:B]).then_inc(rden_ready, 1)
                if jb == 7:
                    dve.wait_ge(z_nat, e + 1)
                    dve.wait_ge(rden_ready, e + 1)
                    for b in range(B):
                        last = nc.vector.scalar_tensor_tensor(x_new[:, b:b + 1, :], nodes(e1)[:, b:b + 1, :], rden[:, b:b + 1],
                                                              x_all[:, bass.ds(e * B + b, 1), :], ALU.mult, ALU.add)
                    last.then_inc(xnew_ready, 1)
                if jb == 8:
                    dve.wait_ge(xnew_ready, GROUPS + e + 1)
                    stats(2 * GROUPS + e, lambda b: x_new[:, b, :])

            def tail2(e, jb):
                if jb == LAG - 2:
                    dve.wait_ge(acc_done, GROUPS + e + 1)
                    dve.wait_ge(self_t, e + 1)
                    nc.vector.tensor_tensor(agg_t[:, :], acc_ps[:, :], pre_t[:, :], ALU.add).then_inc(acc_free, 1)
                if jb == 6:
                    dve.wait_ge(gcn_ps, e + 1)
                    nc.vector.tensor_tensor(h_new[:, :, :], nodes(e0), wide(cols(dinv, e)), ALU.mult).then_inc(gcn_scaled, 1)
                    dve.wait_ge(gcn_scaled, e + 1)
                    nc.vector.scalar_tensor_tensor(x_new[:, :, :], h_new[:, :, :], 0.0, grp(x_all, e), ALU.max, ALU.add).then_inc(xnew_ready, 1)
                if jb == 8:
                    dve.wait_ge(xnew_ready, 2 * GROUPS + e + 1)
                    stats(3 * GROUPS + e, lambda b: x_new[:, b, :])
                if jb == 11:
                    normalise(3 * GROUPS + e, lambda b: x_new[:, b, :], h_new[:, :, :], 2 * GROUPS + e)

            def tail3(e, jb):
                if jb == LAG - 2:
                    dve.wait_ge(acc_done, 2 * GROUPS + e + 1)
                    nc.vector.tensor_copy(agg_t[:, :], acc_ps[:, :]).then_inc(acc_free, 1)
                if jb == LAG:
                    nc.vector.tensor_tensor(den2_s[:, :], den2_acc[:, 0, :], den2_acc[:, 1, :], ALU.add).then_inc(den2_kept, 1)
                if jb == 8:
                    dve.wait_ge(den_nat, e + 1)
                    nc.vector.tensor_copy(SC["den"], e1[:, 0:B]).then_inc(den_ready, 1)
                if jb == 21:
                    dve.wait_ge(c_ready, e + 1)
                    for b in range(B):
                        last = nc.vector.tensor_scalar(h_new[:, b, :], y_nat[:, b, :], SC["c"][:, b:b + 1], 0.0, ALU.mult, ALU.max)
                    last.then_inc(u_made, 1)
                if jb == 28:
                    dve.wait_ge(k_ready, e + 1)
                    dve.wait_ge(out_stored, 16 * (e + 1))
                    for b in range(B):
                        last = nc.vector.scalar_tensor_tensor(x_new[:, b:b + 1, :], h_new[:, b:b + 1, :], SC["k"][:, b:b + 1],
                                                              x_all[:, bass.ds(e * B + b, 1), :], ALU.mult, ALU.add)
                    last.then_inc(out_ready, 1)

            TAILS = {L0: tail0, L1: tail1, L2: tail2, L3: tail3}

            def body(p, g, first):
                for jb in range(BLOCKS):
                    if first and p:
                        TAILS[p - 1](GROUPS - 1, jb)
                    elif not first:
                        TAILS[p](g - 1, jb)
                    if p == L1:
                        unit = g * BLOCKS + jb
                        if jb % B == 0:
                            tile_arrived(dve, p, g, jb // B)
                            if first:
                                dve.wait_ge(exps_ready, 3 * (jb // B + 1))
                                if jb == 0:
                                    dve.wait_ge(acc_done, GROUPS)
                            if not (first and jb < WBUFS):
                                dve.wait_ge(den_mm, (unit - WBUFS) // B + 1 if first else g * (BLOCKS // B) + (jb - WBUFS) // B + 1)
                        nc.vector.scalar_tensor_tensor(att_w[:, jb % WBUFS, :], dst_row[:, bass.ds(g * C, C)], exp_ms[:, jb:jb + 1],
                                                       ring[:, (jb // B) % SLOTS, jb % B, :], ALU.max, ALU.mult).then_inc(w_made, 1)
                        if jb >= 3 and jb % 2:
                            weighted_pair(g, first, jb - 3)
                        elif jb == 1 and not first:
                            weighted_pair(g - 1, False, BLOCKS - 2)
                        continue
                    if p == L2 and first and jb == 0:
                        weighted_pair(GROUPS - 1, False, BLOCKS - 2)
                    dve.wait_ge(hi_ready, (AGG[p] * GROUPS + g) * BLOCKS + jb + 1)
                    if p == L3 and vector_den(jb):
                        q = q_all[:, jb:jb + 1]
                        if first and jb == 5:
                            dve.wait_ge(q_ready, GROUPS - 1)
                        if first and jb // B == GROUPS - 1:
                            dve.wait_ge(q_ready, GROUPS)
                        acc = den2_acc[:, sum(vector_den(u) for u in range(jb)) % 2, :]
                        if jb == 5 and not first:
                            dve.wait_ge(den2_kept, g)
                        if jb <= 6:
                            nc.vector.tensor_scalar(acc, t_ps[jb % LAG][:, :], q, None, ALU.mult)
                        else:
                            dve.wait_ge(lo_ready, (AGG[p] * GROUPS + g) * BLOCKS + jb - 1)
                            nc.vector.scalar_tensor_tensor(acc, t_ps[jb % LAG][:, :], q, acc, ALU.mult, ALU.add)
                    nc.vector.tensor_tensor(t_lo[:, jb % LAG, :], t_ps[jb % LAG][:, :], t_hi[:, jb % LAG, :].bitcast(F32),
                                            ALU.subtract).then_inc(lo_ready, 1)
                    if p == L0 and first and jb % B == 0 and jb // B + 1 < GROUPS:
                        layer0_norm(jb // B + 1)
                        if jb // B + 2 < GROUPS:
                            layer0_stats(jb // B + 2)
                    if p == L0 and first and jb == BLOCKS - 2:
                        dve.wait_ge(w_in, 16 * 11)
                        nc.vector.tensor_tensor(bias_g[:, :], bias[:, 1:3], bias[:, 4:6], ALU.add).then_inc(bias_ready, 1)
                        dve.wait_ge(bias_ready, 1)
                        nc.vector.tensor_scalar(bias_g[:, :], bias_g[:, :], 0.5, None, ALU.mult).then_inc(bias_ready, 1)

            def weighted_pair(g, first, jb):
                dve.wait_ge(w_made, g * BLOCKS + jb + 2)
                if not (first and jb < PBUFS):
                    dve.wait_ge(att_mm, g * BLOCKS + jb + 2 - PBUFS)
                w, q, r = jb % WBUFS, jb % PBUFS, jb % B
                nc.vector.tensor_tensor(att_p[:, q:q + 2, :], att_w[:, w:w + 2, :], ring[:, (jb // B) % SLOTS, r:r + 2, :],
                                        ALU.mult).then_inc(p_made, 2)

            def layer0_stats(k):
                dve.wait_ge(x_in[(k + 1) // 2], 16 if k in (0, GROUPS - 1) else 32)
                stats(k, lambda b: x_all[:, k * B + b, :])

            def layer0_norm(k):
                normalise(k, lambda b: x_all[:, k * B + b, :], nat_a[:, k * B:(k + 1) * B, :], k)

            layer0_stats(0)
            layer0_norm(0)
            layer0_stats(1)
            passes(dve, body)
            for jb in range(BLOCKS):
                tail3(GROUPS - 1, jb)

        @block.gpsimd
        def _(pool):
            g_ = nc.gpsimd
            g_.memset(ident[:, :], 0.0).then_inc(const_step, 1)
            pool.wait_ge(const_step, 1)
            g_.affine_select(out=ident[:, :], in_=ident[:, :], compare_op=ALU.not_equal, fill=1.0, base=0,
                             pattern=[[-1, P]], channel_multiplier=1).then_inc(const_ready, 1)
            g_.memset(avg32[:, :], 1.0 / 32)
            g_.memset(avg64[:, :], 1.0 / 64)
            g_.memset(ones[:, :], 1.0)
            g_.memset(phalf[:, :], 0.5)
            g_.memset(ln_eps[:, :], LN_EPS)
            g_.memset(minus_one[:, :], -1.0)
            g_.memset(mhalf[:, :], -0.5).then_inc(const_ready, 1)
            pool.wait_ge(const_ready, 2)

            def chain(ins):
                pool.drain()

            def layer_rstd(c, chain, nbias_too=False):
                pool.wait_ge(ln_mv, c + 1)
                chain(g_.tensor_tensor(rstd[:, :], mv[:, :, 1], ln_eps[:, :], ALU.add))
                if nbias_too:
                    chain(g_.tensor_tensor(rstd[:, :], rstd[:, :], mhalf[:, 0:B], ALU.pow))
                    chain(g_.tensor_tensor(nbias[:, :], mv[:, :, 0], rstd[:, :], ALU.mult))
                    g_.tensor_scalar(nbias[:, :], nbias[:, :], -1.0, None, ALU.mult).then_inc(ln_rstd, 1)
                else:
                    g_.tensor_tensor(rstd[:, :], rstd[:, :], mhalf[:, 0:B], ALU.pow).then_inc(ln_rstd, 1)

            def split(p, k, chain):
                blk = slice(k * B, (k + 1) * B)
                nat = nat_b if p == L2 else nat_a
                if p == L2:
                    pool.wait_ge(den_mm, (GROUPS * BLOCKS - WBUFS + k) // B + 1)
                pool.wait_ge(hi_split, AGG[p] * GROUPS + k + 1)
                g_.tensor_tensor(src_lo[:, blk, :], nat[:, blk, :], src_hi[:, blk, :].bitcast(F32), ALU.subtract).then_inc(src_ready, 1)

            def scale_source(k):
                blk = slice(k * B, (k + 1) * B)
                pool.wait_ge(ln_done, 2 * GROUPS + k + 1)
                g_.tensor_tensor(nat_b[:, blk, :], nat_b[:, blk, :], wide(dinv[:, blk]), ALU.mult).then_inc(scaled_src, 1)

            def tail0(e, chain):
                layer_rstd(GROUPS + e, chain)

            def tail1(e, chain):
                layer_rstd(2 * GROUPS + e, chain, nbias_too=True)

            def ts(chain, dst, a, s1, s2, o1, o2=None):
                chain(g_.tensor_scalar(SC[dst], SC[a], s1, s2, o1, o2) if o2 is not None else
                      g_.tensor_scalar(SC[dst], SC[a], s1, None, o1))

            def tt(chain, dst, a, b, op):
                chain(g_.tensor_tensor(SC[dst], SC[a], SC[b], op))

            def divide(chain, dst, a, b):
                chain(g_.tensor_tensor(SC["rec"], SC[b], minus_one[:, :], ALU.pow))
                tt(chain, dst, a, "rec", ALU.mult)

            def artanh_arg(chain, src):
                ts(chain, "xc", src, 1.0 - EPS, -1.0 + EPS, ALU.min, ALU.max)
                ts(chain, "inv", "xc", -1.0, 1.0, ALU.mult, ALU.add)
                ts(chain, "one", "xc", 1.0, None, ALU.add)
                divide(chain, "arg", "one", "inv")

            def artanh_series(chain):
                tt(chain, "z2", "xc", "xc", ALU.mult)
                ts(chain, "ser", "z2", 1.0 / 7, 1.0 / 5, ALU.mult, ALU.add)
                tt(chain, "ser", "ser", "z2", ALU.mult)
                ts(chain, "ser", "ser", 1.0 / 3, None, ALU.add)
                tt(chain, "ser", "ser", "z2", ALU.mult)
                ts(chain, "ser", "ser", 1.0, None, ALU.add)
                tt(chain, "ser", "ser", "xc", ALU.mult)
                ts(chain, "mask", "xc", 1.0 / 16, None, ALU.is_lt)

            SC["half"] = phalf[:, :]

            def artanh_end(chain):
                tt(chain, "ath", "ln", "half", ALU.mult)
                tt(chain, "ser", "ser", "ath", ALU.subtract)
                tt(chain, "ser", "ser", "mask", ALU.mult)
                tt(chain, "ath", "ath", "ser", ALU.add)

            def tail2_norm(e, chain):
                layer_rstd(3 * GROUPS + e, chain)

            def tail2a(e, chain):
                pool.wait_ge(xn2_ready, e + 1)
                chain(g_.tensor_tensor(SC["xn"], SC["xn2"], phalf[:, :], ALU.pow))
                ts(chain, "xn", "xn", MIN_NORM, None, ALU.max)
                artanh_arg(chain, "xn")
                g_.tensor_copy(SC["arg"], SC["arg"]).then_inc(ln_arg, 1)

            def tail2b(e, chain):
                artanh_series(chain)
                pool.wait_ge(mx_ready, e + 1)
                chain(g_.tensor_tensor(SC["mxn"], SC["ss"], phalf[:, :], ALU.pow))
                ts(chain, "mxn", "mxn", MIN_NORM, None, ALU.max)
                divide(chain, "z", "mxn", "xn")
                pool.wait_ge(ln_val, e + 1)
                artanh_end(chain)
                tt(chain, "z", "z", "ath", ALU.mult)
                g_.tensor_copy(SC["z"], SC["z"]).then_inc(th_arg, 1)

            def tail2c(e, chain):
                pool.wait_ge(th_val, e + 1)
                divide(chain, "f", "t", "mxn")
                tt(chain, "g", "f", "f", ALU.mult)
                tt(chain, "g", "g", "ss", ALU.mult)
                ts(chain, "g", "g", -1.0, 1.0, ALU.mult, ALU.add)
                ts(chain, "g", "g", EPS, None, ALU.max)
                ts(chain, "g", "g", 0.5, None, ALU.mult)
                chain(g_.tensor_tensor(SC["g"], SC["g"], minus_one[:, :], ALU.pow))
                ts(chain, "c", "g", -1.0, None, ALU.add)
                g_.tensor_copy(cols(q_all, e), SC["c"]).then_inc(q_ready, 1)
                q = SC["c"].rearrange("p (b o) -> p b o", o=1).to_broadcast([P, B, 64])
                pair = q_pair[:, bass.ds(e * B, B), :]
                chain(g_.tensor_copy(pair[:, :, 0:64], q))
                g_.tensor_tensor(pair[:, :, 64:128], q, pair[:, :, 0:64].bitcast(F32), ALU.subtract)
                tt(chain, "f", "f", "g", ALU.mult)
                g_.tensor_tensor(grp(nat_a, e), y_nat[:, :, :], wide(SC["f"]), ALU.mult).then_inc(hyp_src_ready, 1)

            def tail3(e, chain):
                pool.wait_ge(v_ready, e + 1)
                pool.wait_ge(den_ready, e + 1)
                chain(g_.tensor_tensor(SC["mxn"], SC["ss"], phalf[:, :], ALU.pow))
                ts(chain, "sgn", "den", 0.0, None, ALU.is_ge)
                ts(chain, "sgn", "sgn", 2.0, -1.0, ALU.mult, ALU.add)
                tt(chain, "den", "den", "sgn", ALU.mult)
                ts(chain, "den", "den", CLAMP, None, ALU.max)
                divide(chain, "xn", "mxn", "den")
                ts(chain, "xn", "xn", MIN_NORM, None, ALU.max)
                artanh_arg(chain, "xn")
                g_.tensor_copy(SC["arg"], SC["arg"]).then_inc(ln_arg3, 1)
                tt(chain, "den", "den", "xn", ALU.mult)
                artanh_series(chain)
                pool.wait_ge(ln_val3, e + 1)
                artanh_end(chain)
                ts(chain, "ath", "ath", 0.5, None, ALU.mult)
                chain(g_.tensor_tensor(SC["ath"], SC["ath"], cols(rowsum, e), ALU.mult))
                ts(chain, "ath", "ath", ATANH_MAX, -ATANH_MAX, ALU.min, ALU.max)
                divide(chain, "c", "ath", "den")
                g_.tensor_tensor(SC["c"], SC["c"], SC["sgn"], ALU.mult).then_inc(c_ready, 1)
                pool.wait_ge(un2_ready, e + 1)
                chain(g_.tensor_tensor(SC["un"], SC["ss"], phalf[:, :], ALU.pow))
                ts(chain, "un", "un", MIN_NORM, None, ALU.max)
                g_.tensor_copy(SC["un"], SC["un"]).then_inc(th_arg3, 1)
                pool.wait_ge(th_val3, e + 1)
                chain(g_.tensor_tensor(SC["rec"], SC["un"], minus_one[:, :], ALU.pow))
                g_.tensor_tensor(SC["k"], SC["t"], SC["rec"], ALU.mult).then_inc(k_ready, 1)

            def tail2(e, chain):
                tail2_norm(e, chain)
                tail2a(e, chain)
                tail2b(e, chain)
                tail2c(e, chain)

            def looped(tail, count=GROUPS - 1):
                with pool.Fori(0, count) as e:
                    tail(e, chain)

            for k in range(GROUPS):
                layer_rstd(k, chain)
                split(L0, k, chain)
            looped(tail0)
            tail0(GROUPS - 1, chain)
            last = GROUPS - 1
            looped(tail1, last - 1)
            pool.wait_ge(row_summed, (GROUPS - 1) * BLOCKS)
            pool.wait_ge(last_summed, GROUPS * B)
            chain(g_.tensor_tensor(rowsum[:, :], deg_part[:, :, 0], deg_part[:, :, 1], ALU.add))
            for i in range(2, TILES):
                chain(g_.tensor_tensor(rowsum[:, :], rowsum[:, :], deg_part[:, :, i], ALU.add))
            chain(g_.tensor_scalar(dinv[:, :], rowsum[:, :], 1.0, DEG_EPS, ALU.add, ALU.add))
            chain(g_.tensor_tensor(dinv[:, :], dinv[:, :], mhalf[:, :], ALU.pow))
            for k in range(last - 1):
                scale_source(k)
            tail1(last - 1, chain)
            scale_source(last - 1)
            for k in range(3):
                split(L2, k, chain)
            tail1(last, chain)
            for k in range(3, last):
                split(L2, k, chain)
            scale_source(last)
            split(L2, last, chain)
            looped(tail2)
            for k in range(3):
                split(L3, k, chain)
            tail2_norm(last, chain)
            for k in range(3, last):
                split(L3, k, chain)
            tail2a(last, chain)
            tail2b(last, chain)
            tail2c(last, chain)
            split(L3, last, chain)
            looped(tail3)
            tail3(GROUPS - 1, chain)


_INS = ['x', 'adj', 'L0_gnn_W_msg', 'L0_gnn_b_msg', 'L0_gnn_W_ih', 'L0_gnn_W_hh', 'L0_gnn_b_ih', 'L0_gnn_b_hh',
        'L1_gnn_weight', 'L1_gnn_att_src', 'L1_gnn_att_dst', 'L2_gnn_weight', 'L3_gnn_W']
_OUTS = [((4096, 128), 'float32')]


def kernel(**inputs):
    import numpy as _np
    import concourse.bacc as _bacc
    from concourse import mybir as _mybir
    from concourse.bass_utils import run_bass_kernel_spmd as _run

    nc = _bacc.Bacc("TRN2", target_bir_lowering=False, num_devices=1)
    arrays, args = {}, []
    for name in _INS:
        a = _np.ascontiguousarray(inputs[name])
        arrays[f"in_{name}_dram"] = a
        args.append(nc.dram_tensor(f"in_{name}_dram", a.shape, _mybir.dt.from_np(a.dtype), kind="ExternalInput").ap())
    for i, (shape, dtype) in enumerate(_OUTS):
        dt = _mybir.dt.from_np(_np.dtype(dtype))
        args.append(nc.dram_tensor(f"out_{i}_dram", shape, dt, kind="ExternalOutput").ap())
    adjacency_stack(nc, *args)
    r = _run(nc, [arrays], core_ids=[0])
    return r.results[0]["out_0_dram"]
```

```python
import math

import numpy as np
import concourse.bass as bass
from concourse import mybir
from contextlib import ExitStack

F32 = mybir.dt.float32
F32R = mybir.dt.float32r
ALU = mybir.AluOpType
ACT = mybir.ActivationFunctionType
AX = mybir.AxisListType


def adjacency_stack(nc, x, adj, w_msg, b_msg, w_ih, w_hh, b_ih, b_hh, w_att, att_src, att_dst, w_gcn, w_hyp, out):
    P = 128
    N, D = x.shape
    BLOCKS = N // P
    B = 4
    C = B * P
    GROUPS = N // C
    SLOTS = 4
    TILES = N // C
    LAG = 4
    LN_EPS, EPS, MIN_NORM, CLAMP, DEG_EPS = 1e-5, 1e-5, 1e-15, 1e-10, 1e-8
    TOP = float(np.float32(1.0 - EPS))
    ATANH_MAX = 0.5 * math.log((1.0 + TOP) / (1.0 - TOP))
    DBUFS = 4
    WBUFS, PBUFS = 16, 8
    L0, L1, L2, L3 = range(4)
    AGG = {L0: 0, L2: 1, L3: 2}

    ctx = ExitStack()
    with ctx:
        def sb(name, shape, dt=F32):
            return ctx.enter_context(nc.sbuf_tensor(name, shape, dt))

        def pb(name):
            return ctx.enter_context(nc.psum_tensor(name, [P, C], F32))

        def sem(name):
            return ctx.enter_context(nc.semaphore(name))

        x_all = sb("x_all", [P, BLOCKS, D])
        with nc.sbuf_tensor("att_p", [P, PBUFS, C], F32) as att_p:
            pass
        src_hi = sb("src_hi", [P, BLOCKS, D], F32R)
        with nc.sbuf_tensor("att_w", [P, WBUFS, C], F32) as att_w:
            pass
        src_lo = sb("src_lo", [P, BLOCKS, D], F32R)
        t_hi = sb("t_hi", [P, LAG, C], F32R)
        t_lo = sb("t_lo", [P, LAG, C], F32R)
        nat_a = sb("nat_a", [P, BLOCKS, D])
        nat_b = sb("nat_b", [P, BLOCKS, D])
        with nc.sbuf_tensor("dst_row", [P, N], F32) as dst_row:
            pass
        den_scaled = sb("den_scaled", [P, DBUFS, C])
        pool_den = sb("pool_den", [P, C])
        pool_den_s = sb("pool_den_s", [P, C])
        den2_acc = sb("den2_acc", [P, 2, C])
        exp_s = sb("exp_s", [P, BLOCKS])
        exp_ms = sb("exp_ms", [P, BLOCKS])
        deg_part = sb("deg_part", [P, BLOCKS, GROUPS])
        rowsum = sb("rowsum", [P, BLOCKS])
        dinv = sb("dinv", [P, BLOCKS])
        q_all = sb("q_all", [P, BLOCKS])

        ring = sb("ring", [P, SLOTS, B, C])
        junk = sb("junk", [P, 2, C], mybir.dt.bfloat16)

        agg_t = sb("agg_t", [P, C])
        msg_t = sb("msg_t", [P, C])
        r_t = sb("r_t", [P, C])
        z_t = sb("z_t", [P, C])
        n_t = sb("n_t", [P, C])
        pre_t = sb("pre_t", [P, C])
        x_new = sb("x_new", [P, B, D])
        h_new = sb("h_new", [P, B, D])
        h_t = sb("h_t", [P, C])
        y_nat = sb("y_nat", [P, B, D])
        tmp = sb("tmp", [P, B, D])
        den_s = sb("den_s", [P, C])
        st6 = sb("st6", [P, B, 6])
        mv = sb("mv", [P, B, 2])
        rstd = sb("rstd", [P, B])
        nbias = sb("nbias", [P, B])
        rden = sb("rden", [P, B])
        den2_s = sb("den2_s", [P, C])
        scalars = ["xn2", "xn", "ss", "mxn", "arg", "ln", "z2", "ser", "mask", "ath", "z", "t", "f", "g", "den",
                   "sgn", "c", "un", "k", "one", "inv", "xc", "rec"]
        sc = sb("sc", [P, len(scalars), B])
        SC = {n: sc[:, i, :] for i, n in enumerate(scalars)}

        ident = sb("ident", [P, P])
        avg32 = sb("avg32", [P, 1])
        ones = sb("ones", [P, 1])
        mhalf = sb("mhalf", [P, BLOCKS])
        phalf = sb("phalf", [P, B])
        ln_eps = sb("ln_eps", [P, B])
        minus_one = sb("minus_one", [P, B])
        w_nat = sb("w_nat", [P, 8, D])
        w_t = sb("w_t", [P, 8, D])
        w_gcn_s = sb("w_gcn_s", [P, D])
        w_hyp_s = sb("w_hyp_s", [P, D])
        att_cols = sb("att_cols", [P, 2])
        w_src = sb("w_src", [P, 1])
        w_dst = sb("w_dst", [P, P])
        bias = sb("bias", [P, 7])
        bias_g = sb("bias_g", [P, 2])

        t_ps = [pb(f"t_ps{i}") for i in range(LAG)]
        acc_ps = pb("acc_ps")
        e0, e1, e2 = pb("e0"), pb("e1"), pb("e2")
        den_ps = t_ps[3]
        dst_ps = t_ps[0]

        POOL_DEN = [0, 1, 2, 3, 6, 10, 13, 16, 20, 24, 27, 30]
        VECTOR_DEN = [jb for jb in range(BLOCKS) if jb not in POOL_DEN]

        GRU_AT = {
            "hidden": (LAG, 0), "acc": (LAG - 2, 0), "msg": (5, 1), "relu": (6, 5), "rz": (8, 3), "hn": (9, 4),
            "r_tanh": (9, 8), "z_tanh": (10, 9), "r": (10, 10), "rh": (11, 11), "in": (11, 6),
            "npre": (12, 13), "n": (14, 14), "mix": (15, 15), "mixed": (16, 16), "to_nodes": (19, 13), "x_new": (20, 19),
            "keep_x": (21, 20), "stats": (21, 19), "norm": (24, 21), "hT": (27, 18), "h_t": (28, 24), "proj": (30, 21),
            "exps": (31, 26), "att_src": (31, 28)}

        WEIGHTS_AT = 12
        H0_AT = [WEIGHTS_AT + 3 + 2 * k for k in range(GROUPS)]

        def due(step, e, jb):
            return jb == GRU_AT[step][isinstance(e, int)]

        def nodes(ps):
            return ps[:, :].rearrange("p (b d) -> p b d", b=B)

        def grp(t, g):
            return t[:, bass.ds(g * B, B), :]

        def cols(t, g):
            return t[:, bass.ds(g * B, B)]

        def wide(col):
            return col.rearrange("p (b o) -> p b o", o=1).to_broadcast([P, B, D])

        x_in = [sem(f"x_in{i}") for i in range(GROUPS // 2 + 1)]
        w_in = sem("w_in")
        adj_in = [sem(f"adj_in{i}") for i in range(SLOTS)]
        row_summed, last_summed = sem("row_summed"), sem("last_summed")
        t_ready, hi_ready, lo_ready = sem("t_ready"), sem("hi_ready"), sem("lo_ready")
        dst_ready = sem("dst_ready")
        w_made, p_made, pool_p_made, att_mm = sem("w_made"), sem("p_made"), sem("pool_p_made"), sem("att_mm")
        den_mm, q_ready = sem("den_mm"), sem("q_ready")
        den_scaled_ready, pool_den_added = sem("den_scaled_ready"), sem("pool_den_added")
        den2_kept = sem("den2_kept")
        acc_done, acc_free, den_free = sem("acc_done"), sem("acc_free"), sem("den_free")
        const_step, const_ready = sem("const_step"), sem("const_ready")
        wt_ps, wt_ready, wv_ps, wv_ready, bias_ready = (sem(n) for n in ("wt_ps", "wt_ready", "wv_ps", "wv_ready", "bias_ready"))
        ln_mv, ln_rstd, ln_scaled, ln_done = (sem(n) for n in ("ln_mv", "ln_rstd", "ln_scaled", "ln_done"))
        src_ready, hi_split = sem("src_ready"), sem("hi_split")
        h0_ps, h0_t = sem("h0_ps"), sem("h0_t")
        x_kept, xnew_ready = sem("x_kept"), sem("xnew_ready")
        msg_ps, msg_ready, rz_ps, hn_ps, in_ps = (sem(n) for n in ("msg_ps", "msg_ready", "rz_ps", "hn_ps", "in_ps"))
        r_tanh, z_tanh, r_ready, rh_ready, npre_ready, n_ready = (sem(n) for n in (
            "r_tanh", "z_tanh", "r_ready", "rh_ready", "npre_ready", "n_ready"))
        mix_step, gru_out, gru_nat = sem("mix_step"), sem("gru_out"), sem("gru_nat")
        hT_ps, hT_ready = sem("hT_ps"), sem("hT_ready")
        proj_ps, exps_ready, att_src_ready = sem("proj_ps"), sem("exps_ready"), sem("att_src_ready")
        den_ps_ready, rden_ready, z_nat = sem("den_ps_ready"), sem("rden_ready"), sem("z_nat")
        self_ready, self_ps, self_t = sem("self_ready"), sem("self_ps"), sem("self_t")
        gcn_ps, gcn_scaled = sem("gcn_ps"), sem("gcn_scaled")
        mx_ps, mx_ready = sem("mx_ps"), sem("mx_ready")
        ln_arg, ln_val, th_arg, th_val = sem("ln_arg"), sem("ln_val"), sem("th_arg"), sem("th_val")
        v_nat, v_ready, den_nat, den_ready = sem("v_nat"), sem("v_ready"), sem("den_nat"), sem("den_ready")
        ln_arg3, ln_val3, th_arg3, th_val3 = sem("ln_arg3"), sem("ln_val3"), sem("th_arg3"), sem("th_val3")
        c_ready, k_ready = sem("c_ready"), sem("k_ready")
        out_ready, out_stored = sem("out_ready"), sem("out_stored")
        hyp_src_ready = sem("hyp_src_ready")
        scaled_src = sem("scaled_src")
        xn2_ready, u_made, un2_ready = sem("xn2_ready"), sem("u_made"), sem("un2_ready")

        block = ctx.enter_context(nc.Block())

        def passes(engine, body, apart=False):
            for p in (L0, L1, L2, L3):
                body(p, 0, True)
                last = GROUPS - (apart and p == L1)
                with engine.Fori(1, last) as g:
                    body(p, g, False)
                if last < GROUPS:
                    body(p, last, False)

        @block.sync
        def _(sp):
            def load_x(b):
                sp.dma_start(grp(x_all, b), x[b * C:(b + 1) * C, :].rearrange("(b p) d -> p b d", p=P)).then_inc(x_in[(b + 1) // 2], 16)

            def body(p, g, first):
                for k in range(TILES):
                    s, wrap = k % SLOTS, k < SLOTS
                    q = p - 1 if first and wrap else p
                    done = (TILES * GROUPS if first and wrap else TILES * g) + k - SLOTS + 1
                    if q == L0:
                        sp.wait_ge(hi_ready, done * B)
                    elif q in AGG:
                        sp.wait_ge(t_ready, (AGG[q] * TILES * GROUPS + done) * B)
                    elif q == L1:
                        sp.wait_ge(p_made, done * B)
                        sp.wait_ge(pool_p_made, done * B)
                        if p == L1 and not (isinstance(g, int) and g == GROUPS - 1 and not wrap):
                            sp.wait_ge(row_summed, done * B)
                    row, col = (k, g) if p == L1 else (g, k)
                    tile = adj[bass.ds(row * C, C), bass.ds(col * C, C)]
                    sp.dma_start(ring[:, s, :, :], tile.rearrange("(b p) c -> p b c", p=P)).then_inc(adj_in[s], 16)
                    if p == L0 and first and k < GROUPS // 2:
                        for b in range(2 * k + 1, min(2 * k + 3, GROUPS)):
                            load_x(b)

            sp.sem_inc(out_stored, 16)
            load_x(0)
            passes(sp, body, apart=True)
            sp.wait_ge(out_stored, 16 * (GROUPS + 1))

        def tile_arrived(engine, p, g, k):
            engine.wait_ge(adj_in[k % SLOTS], 16 * ((p * GROUPS + g) * (TILES // SLOTS) + k // SLOTS + 1))

        @block.tensor
        def _(pe):
            def weights():
                pe.wait_ge(w_in, 16 * 11)
                for i in range(8):
                    last = nc.tensor.transpose((e0 if i < 4 else e1)[:, bass.ds((i % 4) * P, P)], w_nat[:, i, :], ident[:, :])
                last.then_inc(wt_ps, 1)
                nc.tensor.matmul(e2[:, 0:1], w_nat[:, 7, :], att_cols[:, 0:1], start=True, stop=True)
                nc.tensor.matmul(e2[:, P:2 * P], w_nat[:, 7, :], att_cols[:, 1:2].to_broadcast([P, P]),
                                 start=True, stop=True).then_inc(wv_ps, 1)

            def transpose4(dst, src):
                for b in range(B):
                    last = nc.tensor.transpose(dst[:, b * P:(b + 1) * P], src(b), ident[:, :])
                return last

            def hT(c):
                pe.wait_ge(ln_done, c + 1)
                transpose4(e1, lambda b: h_new[:, b, :]).then_inc(hT_ps, 1)

            def tail0(e, jb):
                if due("hidden", e, jb):
                    pe.wait_ge(h0_t, GROUPS)
                    hid = nat_b_t(e)
                    nc.tensor.matmul(e0[:, :], w_t[:, 4, :], hid, start=True, stop=False)
                    nc.tensor.matmul(e1[:, :], w_t[:, 5, :], hid, start=True, stop=False)
                if due("msg", e, jb):
                    pe.wait_ge(acc_free, e + 1)
                    nc.tensor.matmul(e2[:, :], w_t[:, 0, :], agg_t[:, :], start=True, stop=True).then_inc(msg_ps, 1)
                if due("rz", e, jb):
                    pe.wait_ge(msg_ready, e + 1)
                    nc.tensor.matmul(e0[:, :], w_t[:, 1, :], msg_t[:, :], start=False, stop=True).then_inc(rz_ps, 1)
                    nc.tensor.matmul(e1[:, :], w_t[:, 2, :], msg_t[:, :], start=False, stop=True).then_inc(rz_ps, 1)
                if due("hn", e, jb):
                    nc.tensor.matmul(e2[:, :], w_t[:, 6, :], nat_b_t(e), start=True, stop=True).then_inc(hn_ps, 1)
                if due("in", e, jb):
                    pe.wait_ge(r_tanh, e + 1)
                    nc.tensor.matmul(e0[:, :], w_t[:, 3, :], msg_t[:, :], start=True, stop=True).then_inc(in_ps, 1)
                if due("to_nodes", e, jb):
                    pe.wait_ge(gru_out, e + 1)
                    pe.wait_ge(z_tanh, e + 1)
                    transpose4(e1, lambda b: n_t[:, b * P:(b + 1) * P]).then_inc(gru_nat, 1)
                if due("hT", e, jb):
                    hT(GROUPS + e)
                if due("proj", e, jb):
                    pe.wait_ge(hT_ready, e + 1)
                    pe.wait_ge(npre_ready, e + 1)
                    for b in range(B):
                        nc.tensor.matmul(e0[:, b * P:(b + 1) * P], h_t[:, b * P:(b + 1) * P], w_t[:, 7, :], start=True, stop=True)
                    nc.tensor.matmul(e1[:, :], w_dst[:, :], h_t[:, :], start=True, stop=True)
                    for b in range(B):
                        last = nc.tensor.matmul(e2[:, b:b + 1], h_t[:, b * P:(b + 1) * P], w_src[:, :], start=True, stop=True)
                    last.then_inc(proj_ps, 1)

            def nat_b_t(e):
                return nat_b[:, bass.ds(e * B, B), :].rearrange("p b d -> p (b d)")

            def tail1(e, jb):
                if jb == (3 if isinstance(e, int) else 2):
                    pe.wait_ge(acc_free, GROUPS + e + 1)
                    pe.wait_ge(den_free, e + 1)
                    for b in range(B):
                        last = nc.tensor.matmul(e0[:, b:b + 1], den_s[:, b * P:(b + 1) * P], avg32[:, :], start=True, stop=True)
                    last.then_inc(den_ps_ready, 1)
                    transpose4(e1, lambda b: agg_t[:, b * P:(b + 1) * P]).then_inc(z_nat, 1)

            def tail2(e, jb):
                if jb == 5:
                    pe.wait_ge(acc_free, 2 * GROUPS + e + 1)
                    for b in range(B):
                        last = nc.tensor.matmul(e0[:, b * P:(b + 1) * P], agg_t[:, b * P:(b + 1) * P], w_gcn_s[:, :], start=True, stop=True)
                    last.then_inc(gcn_ps, 1)
                if jb == 14:
                    hT(3 * GROUPS + e)
                if jb == 17:
                    pe.wait_ge(hT_ready, GROUPS + e + 1)
                    for b in range(B):
                        last = nc.tensor.matmul(e0[:, b * P:(b + 1) * P], h_t[:, b * P:(b + 1) * P], w_hyp_s[:, :], start=True, stop=True)
                    last.then_inc(mx_ps, 1)

            def tail3(e, jb):
                if jb == 6:
                    pe.wait_ge(acc_free, 3 * GROUPS + e + 1)
                    transpose4(e0, lambda b: agg_t[:, b * P:(b + 1) * P]).then_inc(v_nat, 1)
                if jb == 7:
                    pe.wait_ge(pool_den_added, (e + 1) * len(POOL_DEN))
                    pe.wait_ge(den2_kept, e + 1)
                    for b in range(B):
                        nc.tensor.matmul(e1[:, b:b + 1], pool_den_s[:, b * P:(b + 1) * P], ones[:, :], start=True, stop=False)
                        last = nc.tensor.matmul(e1[:, b:b + 1], den2_s[:, b * P:(b + 1) * P], ones[:, :], start=False, stop=True)
                    last.then_inc(den_nat, 1)

            TAILS = {L0: tail0, L1: tail1, L2: tail2, L3: tail3}

            def products(p, g, jb):
                unit = (AGG[p] * GROUPS + g) * BLOCKS + jb
                pe.wait_ge(lo_ready, unit + 1)
                if jb == 0 and not (p == L0 and isinstance(g, int)):
                    pe.wait_ge(acc_free, p * GROUPS + g)
                if jb % B == 0 and (jb == BLOCKS - LAG or isinstance(g, int) and g == 0):
                    pe.wait_ge(src_ready, AGG[p] * GROUPS + jb // B + 1)
                b = jb % LAG
                first, last = jb == 0, jb == BLOCKS - 1
                nc.tensor.matmul(acc_ps[:, :], src_hi[:, jb, :], t_hi[:, b, :], start=first, stop=False)
                nc.tensor.matmul(acc_ps[:, :], src_lo[:, jb, :], t_hi[:, b, :], start=False, stop=False)
                mm = nc.tensor.matmul(acc_ps[:, :], src_hi[:, jb, :], t_lo[:, b, :], start=False, stop=last)
                if last:
                    mm.then_inc(acc_done, 1)

            def body(p, g, first):
                if p == L1:
                    for jb in range(BLOCKS):
                        if first:
                            tail0(GROUPS - 1, jb)
                        else:
                            tail1(g - 1, jb)
                        if jb == 0:
                            pe.wait_ge(acc_free, GROUPS + g)
                        if first and jb % B == 0:
                            pe.wait_ge(att_src_ready, jb // B + 1)
                        if jb % B == 0:
                            pe.wait_ge(pool_p_made, g * BLOCKS + jb + B)
                        if jb % B == 1:
                            pe.wait_ge(p_made, g * BLOCKS + jb + B - 1)
                        nc.tensor.matmul(acc_ps[:, :], nat_a[:, jb, :], att_p[:, jb % PBUFS, :], start=jb == 0,
                                         stop=jb == BLOCKS - 1).then_inc(att_mm, 1)
                        if jb == B - 1 and not first:
                            pe.wait_ge(den_free, g)
                        if jb % B == B - 1:
                            for q in range(B):
                                j = jb - B + 1 + q
                                last = nc.tensor.matmul(den_ps[32 * q:32 * q + 32, :], exp_s[:, j:j + 1].to_broadcast([P, 32]),
                                                        att_w[:, j % WBUFS, :], start=jb == B - 1, stop=jb == BLOCKS - 1)
                            last.then_inc(den_mm, 1)
                    return
                for jb in range(BLOCKS):
                    if first:
                        if p == L0:
                            if jb == WEIGHTS_AT:
                                weights()
                            if jb in H0_AT:
                                k = H0_AT.index(jb)
                                pe.wait_ge(ln_done, k + 1)
                                if k > 1:
                                    pe.wait_ge(h0_t, k - 1)
                                elif k == 0:
                                    pe.wait_ge(wt_ready, 2)
                                transpose4((e0, e1)[k % 2], lambda b: nat_a[:, k * B + b, :]).then_inc(h0_ps, 1)
                        elif p == L2:
                            tail1(GROUPS - 1, jb)
                        else:
                            tail2(GROUPS - 1, jb)
                    else:
                        TAILS[p](g - 1, jb)
                    if p == L2 and jb == (20 if first else LAG):
                        pe.wait_ge(self_ready, g + 1)
                        transpose4(e1, lambda b: tmp[:, b, :]).then_inc(self_ps, 1)
                    if jb >= LAG:
                        products(p, g, jb - LAG)
                    elif not first:
                        products(p, g - 1, BLOCKS - LAG + jb)
                    elif p == L3:
                        products(L2, GROUPS - 1, BLOCKS - LAG + jb)
                    if jb % B == 0:
                        tile_arrived(pe, p, g, jb // B)
                    if p == L2 and first and jb == 3:
                        pe.wait_ge(den_free, GROUPS)
                    for b in range(B):
                        last = nc.tensor.transpose(t_ps[jb % LAG][:, b * P:(b + 1) * P],
                                                   ring[:, (jb // B) % SLOTS, b, (jb % B) * P:(jb % B + 1) * P], ident[:, :])
                    last.then_inc(t_ready, 1)

            def flush(p):
                for jb in range(BLOCKS - LAG, BLOCKS):
                    products(p, GROUPS - 1, jb)

            pe.wait_ge(const_ready, 1)
            for p in (L0, L1, L2, L3):
                body(p, 0, True)
                with pe.Fori(1, GROUPS) as g:
                    body(p, g, False)
                if p in (L0, L3):
                    flush(p)
            for jb in range(BLOCKS):
                tail3(GROUPS - 1, jb)

        @block.scalar
        def _(act):
            def load(dst, src):
                act.dma_start(dst, src).then_inc(w_in, 16)

            load(w_nat[:, 0, :], w_msg)
            load(w_nat[:, 1:4, :], w_ih.rearrange("(t p) d -> p t d", p=P))
            load(w_nat[:, 4:7, :], w_hh.rearrange("(t p) d -> p t d", p=P))
            load(w_nat[:, 7, :], w_att)

            def weights():
                act.wait_ge(wt_ps, 1)
                nc.scalar.activation(w_t[:, 0:4, :], nodes(e0), ACT.Copy).then_inc(wt_ready, 1)
                nc.scalar.activation(w_t[:, 4:8, :], nodes(e1), ACT.Copy).then_inc(wt_ready, 1)
                act.wait_ge(wv_ps, 1)
                nc.scalar.activation(w_src[:, :], e2[:, 0:1], ACT.Copy).then_inc(wv_ready, 1)
                nc.scalar.activation(w_dst[:, :], e2[:, P:2 * P], ACT.Copy).then_inc(wv_ready, 1)

            def hT(c):
                act.wait_ge(hT_ps, c + 1)
                nc.scalar.activation(h_t[:, :], e1[:, :], ACT.Copy).then_inc(hT_ready, 1)

            def tail0(e, jb):
                if due("relu", e, jb):
                    act.wait_ge(msg_ps, e + 1)
                    nc.scalar.activation(msg_t[:, :], e2[:, :], ACT.Relu, bias=bias[:, 0:1]).then_inc(msg_ready, 1)
                if due("r_tanh", e, jb):
                    act.wait_ge(rz_ps, 2 * e + 1)
                    nc.scalar.activation(r_t[:, :], e0[:, :], ACT.Tanh, bias=bias_g[:, 0:1], scale=0.5).then_inc(r_tanh, 1)
                if due("z_tanh", e, jb):
                    act.wait_ge(rz_ps, 2 * e + 2)
                    nc.scalar.activation(z_t[:, :], e1[:, :], ACT.Tanh, bias=bias_g[:, 1:2], scale=0.5).then_inc(z_tanh, 1)
                if due("n", e, jb):
                    act.wait_ge(npre_ready, e + 1)
                    nc.scalar.activation(n_t[:, :], pre_t[:, :], ACT.Tanh, bias=bias[:, 3:4]).then_inc(n_ready, 1)
                if due("keep_x", e, jb):
                    keep_x(L0, e)
                if due("h_t", e, jb):
                    hT(e)
                if due("exps", e, jb):
                    act.wait_ge(proj_ps, e + 1)
                    nc.scalar.activation(cols(exp_s, e), e2[:, 0:B], ACT.Exp).then_inc(exps_ready, 1)
                    nc.scalar.activation(cols(exp_ms, e), e2[:, 0:B], ACT.Exp, scale=-0.8).then_inc(exps_ready, 1)
                    nc.scalar.activation(dst_row[:, bass.ds(e * C, C)], e1[:, :], ACT.Exp, scale=0.8).then_inc(exps_ready, 1)

            def tail1(e, jb):
                if jb == 0:
                    act.wait_ge(att_mm, (e + 1) * BLOCKS)
                    nc.scalar.activation(agg_t[:, :], acc_ps[:, :], ACT.Copy).then_inc(acc_free, 1)
                    act.wait_ge(den_mm, (e + 1) * (BLOCKS // B))
                    nc.scalar.activation(den_s[:, :], den_ps[:, :], ACT.Copy).then_inc(den_free, 1)
                if jb == 11:
                    keep_x(L1, e)
                if jb == 13:
                    act.wait_ge(ln_rstd, 2 * GROUPS + e + 1)
                    for b in range(B):
                        last = nc.scalar.activation(nat_b[:, bass.ds(e * B + b, 1), :], x_new[:, b:b + 1, :], ACT.Relu,
                                                    bias=nbias[:, b:b + 1], scale=rstd[:, b:b + 1])
                    last.then_inc(ln_done, 1)

            def keep_x(layer, e):
                act.wait_ge(xnew_ready, layer * GROUPS + e + 1)
                nc.scalar.activation(grp(x_all, e), x_new[:, :, :], ACT.Copy).then_inc(x_kept, 1)

            def squares(dst, src):
                for b in range(B):
                    last = nc.scalar.activation(junk[:, 0, b * D:(b + 1) * D], src[:, b, :], ACT.Square, accum_out=SC[dst][:, b:b + 1])
                return last

            def tail2(e, jb):
                if jb == 10:
                    keep_x(L2, e)
                if jb == 13:
                    act.wait_ge(ln_done, 3 * GROUPS + e + 1)
                    squares("xn2", h_new).then_inc(xn2_ready, 1)
                if jb == 15:
                    hT(GROUPS + e)
                if jb == 18:
                    act.wait_ge(mx_ps, e + 1)
                    nc.scalar.activation(y_nat[:, :, :], nodes(e0), ACT.Copy)
                    squares("ss", nodes(e0)).then_inc(mx_ready, 1)
                if jb == 17:
                    act.wait_ge(ln_arg, e + 1)
                    nc.scalar.activation(SC["ln"], SC["arg"], ACT.Ln).then_inc(ln_val, 1)
                if jb == 22:
                    act.wait_ge(th_arg, e + 1)
                    nc.scalar.activation(SC["t"], SC["z"], ACT.Tanh).then_inc(th_val, 1)

            def tail3(e, jb):
                if jb == 7:
                    act.wait_ge(v_nat, e + 1)
                    nc.scalar.activation(y_nat[:, :, :], nodes(e0), ACT.Copy)
                    squares("ss", nodes(e0)).then_inc(v_ready, 1)
                if jb == 15:
                    act.wait_ge(ln_arg3, e + 1)
                    nc.scalar.activation(SC["ln"], SC["arg"], ACT.Ln).then_inc(ln_val3, 1)
                if jb == 24:
                    act.wait_ge(u_made, e + 1)
                    squares("ss", h_new).then_inc(un2_ready, 1)
                if jb == 26:
                    act.wait_ge(th_arg3, e + 1)
                    nc.scalar.activation(SC["t"], SC["un"], ACT.Tanh).then_inc(th_val3, 1)
                if jb == BLOCKS - 1:
                    act.wait_ge(out_ready, e + 1)
                    act.dma_start(out[bass.ds(e * C, C), :].rearrange("(b p) d -> p b d", p=P), x_new[:, :, :]).then_inc(out_stored, 16)

            TAILS = {L0: tail0, L1: tail1, L2: tail2, L3: tail3}

            def source_hi(p, k):
                blk = slice(k * B, (k + 1) * B)
                if p == L0:
                    act.wait_ge(ln_done, k + 1)
                elif p == L2:
                    act.wait_ge(scaled_src, k + 1)
                    act.wait_ge(att_mm, GROUPS * BLOCKS - PBUFS + k + 1)
                else:
                    act.wait_ge(hyp_src_ready, k + 1)
                    act.wait_ge(t_ready, (AGG[L2] * GROUPS + GROUPS - 1) * BLOCKS + (k + 1) * B + LAG)
                nc.scalar.activation(src_hi[:, blk, :], (nat_b if p == L2 else nat_a)[:, blk, :], ACT.Copy).then_inc(hi_split, 1)

            def body(p, g, first):
                for jb in range(BLOCKS):
                    if p == L1 and jb == 0:
                        if first:
                            act.wait_ge(lo_ready, GROUPS * BLOCKS)
                        else:
                            act.wait_ge(w_made, g * BLOCKS)
                        nc.scalar.activation(dst_ps[:, :], dst_row[:, bass.ds(g * C, C)], ACT.Copy).then_inc(dst_ready, 1)
                    if first and p:
                        TAILS[p - 1](GROUPS - 1, jb)
                    elif not first:
                        TAILS[p](g - 1, jb)
                    if p == L2 and jb == (19 if first else 2):
                        if first:
                            act.wait_ge(scaled_src, 1)
                        nc.scalar.activation(tmp[:, :, :], grp(nat_b, g), ACT.Copy).then_inc(self_ready, 1)
                    if p == L2 and jb == (21 if first else 5):
                        if not first:
                            act.wait_ge(acc_free, 2 * GROUPS + g)
                        act.wait_ge(self_ps, g + 1)
                        nc.scalar.activation(pre_t[:, :], e1[:, :], ACT.Copy).then_inc(self_t, 1)
                    if p == L1 and not (isinstance(g, int) and g == GROUPS - 1):
                        if jb % B == 0:
                            tile_arrived(act, p, g, jb // B)
                        if first and jb < 2:
                            act.wait_ge(last_summed, GROUPS * B + jb - 1)
                        else:
                            act.wait_ge(row_summed, g * BLOCKS + jb - 1)
                        nc.scalar.activation(junk[:, jb % 2, :], ring[:, (jb // B) % SLOTS, jb % B, :], ACT.Copy,
                                             accum_out=deg_part[:, jb, bass.ds(g, 1)]).then_inc(row_summed, 1)
                    if p == L0 and jb // B == TILES - 1:
                        if jb % B == 0:
                            tile_arrived(act, p, g, TILES - 1)
                        if not (first and jb % B < 2):
                            act.wait_ge(last_summed, g * B + jb % B - 1)
                        nc.scalar.activation(junk[:, jb % 2, :], ring[:, (TILES - 1) % SLOTS, jb % B, :], ACT.Copy,
                                             accum_out=deg_part[:, bass.ds(g * B + jb % B, 1), TILES - 1]).then_inc(last_summed, 1)
                    if p == L1:
                        continue
                    if p == L0 and first and jb % B == 1 and jb // B + 1 < GROUPS:
                        source_hi(p, jb // B + 1)
                    if first and p in (L2, L3) and (jb % 2 == 0 and jb // 2 < GROUPS - 1 or jb == (15 if p == L2 else 28)):
                        source_hi(p, min(jb // 2, GROUPS - 1))
                    act.wait_ge(t_ready, (AGG[p] * GROUPS + g) * BLOCKS + jb + 1)
                    if p == L3 and jb in POOL_DEN:
                        i = POOL_DEN.index(jb)
                        if first and i == 0:
                            act.wait_ge(q_ready, GROUPS - 1)
                        if first and jb == min(u for u in POOL_DEN if u >= BLOCKS - B):
                            act.wait_ge(q_ready, GROUPS)
                        if not (first and i < DBUFS):
                            act.wait_ge(pool_den_added, g * len(POOL_DEN) + i + 1 - DBUFS)
                        nc.scalar.activation(den_scaled[:, i % DBUFS, :], t_ps[jb % LAG][:, :], ACT.Copy,
                                             scale=q_all[:, jb:jb + 1]).then_inc(den_scaled_ready, 1)
                    nc.scalar.activation(t_hi[:, jb % LAG, :], t_ps[jb % LAG][:, :], ACT.Copy).then_inc(hi_ready, 1)
                    if p == L0 and first and jb == WEIGHTS_AT + 1:
                        weights()
                    if p == L0 and first and jb in H0_AT:
                        k = H0_AT.index(jb)
                        act.wait_ge(h0_ps, k + 1)
                        nc.scalar.activation(nat_b[:, k * B:(k + 1) * B, :], nodes((e0, e1)[k % 2]), ACT.Copy).then_inc(h0_t, 1)

            source_hi(L0, 0)
            load(w_gcn_s[:, :], w_gcn)
            load(w_hyp_s[:, :], w_hyp)
            with nc.allow_non_contiguous_dma(reason="a few hundred floats, one per partition"):
                load(att_cols[:, 0:1], att_src.rearrange("o d -> d o"))
                load(att_cols[:, 1:2], att_dst.rearrange("o d -> d o"))
                load(bias[:, 0:1], b_msg.rearrange("(o d) -> d o", o=1))
                load(bias[:, 1:4], b_ih.rearrange("(t d) -> d t", t=3))
                load(bias[:, 4:7], b_hh.rearrange("(t d) -> d t", t=3))
            passes(act, body, apart=True)
            for jb in range(BLOCKS):
                tail3(GROUPS - 1, jb)

        @block.vector
        def _(dve):
            def stats(c, src):
                for b in range(B):
                    last = nc.vector.bn_stats(st6[:, b, :], src(b))
                dve.drain()
                for b in range(B):
                    last = nc.vector.bn_aggr(mv[:, b, :], st6[:, b, :])
                last.then_inc(ln_mv, 1)

            def normalise(c, src, dst, n):
                dve.wait_ge(ln_rstd, c + 1)
                for b in range(B):
                    last = nc.vector.tensor_scalar(h_new[:, b, :], src(b), mv[:, b, 0:1], rstd[:, b:b + 1], ALU.subtract, ALU.mult)
                last.then_inc(ln_scaled, 1)
                dve.wait_ge(ln_scaled, n + 1)
                nc.vector.tensor_scalar(dst, h_new[:, :, :], 0.0, None, ALU.max).then_inc(ln_done, 1)

            def tail0(e, jb):
                if due("acc", e, jb):
                    dve.wait_ge(acc_done, e + 1)
                    nc.vector.tensor_copy(agg_t[:, :], acc_ps[:, :]).then_inc(acc_free, 1)
                if due("r", e, jb):
                    dve.wait_ge(r_tanh, e + 1)
                    nc.vector.tensor_scalar(r_t[:, :], r_t[:, :], 0.5, 0.5, ALU.mult, ALU.add).then_inc(r_ready, 1)
                if due("rh", e, jb):
                    dve.wait_ge(r_ready, e + 1)
                    dve.wait_ge(hn_ps, e + 1)
                    nc.vector.scalar_tensor_tensor(pre_t[:, :], e2[:, :], bias[:, 6:7], r_t[:, :], ALU.add, ALU.mult).then_inc(rh_ready, 1)
                if due("npre", e, jb):
                    dve.wait_ge(rh_ready, e + 1)
                    dve.wait_ge(in_ps, e + 1)
                    nc.vector.tensor_tensor(pre_t[:, :], e0[:, :], pre_t[:, :], ALU.add).then_inc(npre_ready, 1)
                if due("mix", e, jb):
                    dve.wait_ge(n_ready, e + 1)
                    hid = nat_b[:, bass.ds(e * B, B), :].rearrange("p b d -> p (b d)")
                    nc.vector.tensor_tensor(msg_t[:, :], hid, n_t[:, :], ALU.subtract).then_inc(mix_step, 1)
                    dve.wait_ge(mix_step, 2 * e + 1)
                    nc.vector.scalar_tensor_tensor(msg_t[:, :], z_t[:, :], 1.0, msg_t[:, :], ALU.add, ALU.mult).then_inc(mix_step, 1)
                if due("mixed", e, jb):
                    dve.wait_ge(mix_step, 2 * e + 2)
                    nc.vector.scalar_tensor_tensor(n_t[:, :], msg_t[:, :], 0.5, n_t[:, :], ALU.mult, ALU.add).then_inc(gru_out, 1)
                if due("x_new", e, jb):
                    dve.wait_ge(gru_nat, e + 1)
                    nc.vector.tensor_tensor(x_new[:, :, :], nodes(e1), grp(x_all, e), ALU.add).then_inc(xnew_ready, 1)
                if due("stats", e, jb):
                    dve.wait_ge(xnew_ready, e + 1)
                    stats(GROUPS + e, lambda b: x_new[:, b, :])
                if due("norm", e, jb):
                    normalise(GROUPS + e, lambda b: x_new[:, b, :], h_new[:, :, :], GROUPS + e)
                if due("att_src", e, jb):
                    dve.wait_ge(exps_ready, 3 * e + 1)
                    nc.vector.tensor_tensor(grp(nat_a, e), nodes(e0), wide(cols(exp_s, e)), ALU.mult).then_inc(att_src_ready, 1)

            def tail1(e, jb):
                if jb == 9:
                    dve.wait_ge(den_ps_ready, e + 1)
                    nc.vector.reciprocal(rden[:, :], e0[:, 0:B]).then_inc(rden_ready, 1)
                if jb == 10:
                    dve.wait_ge(z_nat, e + 1)
                    dve.wait_ge(rden_ready, e + 1)
                    for b in range(B):
                        last = nc.vector.scalar_tensor_tensor(x_new[:, b:b + 1, :], nodes(e1)[:, b:b + 1, :], rden[:, b:b + 1],
                                                              x_all[:, bass.ds(e * B + b, 1), :], ALU.mult, ALU.add)
                    last.then_inc(xnew_ready, 1)
                if jb == 11:
                    dve.wait_ge(xnew_ready, GROUPS + e + 1)
                    stats(2 * GROUPS + e, lambda b: x_new[:, b, :])

            def tail2(e, jb):
                if jb == LAG - 2:
                    dve.wait_ge(acc_done, GROUPS + e + 1)
                    dve.wait_ge(self_t, e + 1)
                    nc.vector.tensor_tensor(agg_t[:, :], acc_ps[:, :], pre_t[:, :], ALU.add).then_inc(acc_free, 1)
                if jb == 6:
                    dve.wait_ge(gcn_ps, e + 1)
                    nc.vector.tensor_tensor(h_new[:, :, :], nodes(e0), wide(cols(dinv, e)), ALU.mult).then_inc(gcn_scaled, 1)
                    dve.wait_ge(gcn_scaled, e + 1)
                    nc.vector.scalar_tensor_tensor(x_new[:, :, :], h_new[:, :, :], 0.0, grp(x_all, e), ALU.max, ALU.add).then_inc(xnew_ready, 1)
                if jb == 8:
                    dve.wait_ge(xnew_ready, 2 * GROUPS + e + 1)
                    stats(3 * GROUPS + e, lambda b: x_new[:, b, :])
                if jb == 11:
                    normalise(3 * GROUPS + e, lambda b: x_new[:, b, :], h_new[:, :, :], 2 * GROUPS + e)

            def tail3(e, jb):
                if jb == LAG - 2:
                    dve.wait_ge(acc_done, 2 * GROUPS + e + 1)
                    nc.vector.tensor_copy(agg_t[:, :], acc_ps[:, :]).then_inc(acc_free, 1)
                if jb == LAG:
                    dve.wait_ge(lo_ready, (AGG[L3] * GROUPS + e + 1) * BLOCKS)
                    nc.vector.tensor_tensor(den2_s[:, :], den2_acc[:, 0, :], den2_acc[:, 1, :], ALU.add).then_inc(den2_kept, 1)
                    dve.wait_ge(den2_kept, e + 1)
                if jb == 8:
                    dve.wait_ge(den_nat, e + 1)
                    nc.vector.tensor_copy(SC["den"], e1[:, 0:B]).then_inc(den_ready, 1)
                if jb == 22:
                    dve.wait_ge(c_ready, e + 1)
                    for b in range(B):
                        last = nc.vector.tensor_scalar(h_new[:, b, :], y_nat[:, b, :], SC["c"][:, b:b + 1], 0.0, ALU.mult, ALU.max)
                    last.then_inc(u_made, 1)
                if jb == 29:
                    dve.wait_ge(k_ready, e + 1)
                    dve.wait_ge(out_stored, 16 * (e + 1))
                    for b in range(B):
                        last = nc.vector.scalar_tensor_tensor(x_new[:, b:b + 1, :], h_new[:, b:b + 1, :], SC["k"][:, b:b + 1],
                                                              x_all[:, bass.ds(e * B + b, 1), :], ALU.mult, ALU.add)
                    last.then_inc(out_ready, 1)

            TAILS = {L0: tail0, L1: tail1, L2: tail2, L3: tail3}

            def body(p, g, first):
                for jb in range(BLOCKS):
                    if first and p:
                        TAILS[p - 1](GROUPS - 1, jb)
                    elif not first:
                        TAILS[p](g - 1, jb)
                    if p == L1:
                        unit = g * BLOCKS + jb
                        if jb % B == 0:
                            tile_arrived(dve, p, g, jb // B)
                            if first:
                                dve.wait_ge(exps_ready, 3 * (jb // B + 1))
                                if jb == 0:
                                    dve.wait_ge(acc_done, GROUPS)
                            if not (first and jb < WBUFS):
                                dve.wait_ge(den_mm, (unit - WBUFS) // B + 1 if first else g * (BLOCKS // B) + (jb - WBUFS) // B + 1)
                        dst = dst_row[:, bass.ds(g * C, C)]
                        if jb >= B:
                            dst = dst_ps[:, :]
                            if jb == B:
                                dve.wait_ge(dst_ready, g + 1)
                        nc.vector.scalar_tensor_tensor(att_w[:, jb % WBUFS, :], dst, exp_ms[:, jb:jb + 1],
                                                       ring[:, (jb // B) % SLOTS, jb % B, :], ALU.max, ALU.mult).then_inc(w_made, 1)
                        if jb >= B and jb % B == 0:
                            weighted(g, jb - B)
                        elif jb == 0 and not first:
                            weighted(g - 1, BLOCKS - B)
                        continue
                    if p == L2 and first and jb == 0:
                        weighted(GROUPS - 1, BLOCKS - B)
                    dve.wait_ge(hi_ready, (AGG[p] * GROUPS + g) * BLOCKS + jb + 1)
                    if p == L3 and jb in VECTOR_DEN:
                        i = VECTOR_DEN.index(jb)
                        q = q_all[:, jb:jb + 1]
                        acc = den2_acc[:, i % 2, :]
                        if first and i == 0:
                            dve.wait_ge(q_ready, GROUPS - 1)
                        if first and jb == min(u for u in VECTOR_DEN if u >= BLOCKS - B):
                            dve.wait_ge(q_ready, GROUPS)
                        if i < 2:
                            nc.vector.tensor_scalar(acc, t_ps[jb % LAG][:, :], q, None, ALU.mult)
                        else:
                            dve.wait_ge(lo_ready, (AGG[p] * GROUPS + g) * BLOCKS + VECTOR_DEN[i - 2] + 1)
                            nc.vector.scalar_tensor_tensor(acc, t_ps[jb % LAG][:, :], q, acc, ALU.mult, ALU.add)
                    nc.vector.tensor_tensor(t_lo[:, jb % LAG, :], t_ps[jb % LAG][:, :], t_hi[:, jb % LAG, :].bitcast(F32),
                                            ALU.subtract).then_inc(lo_ready, 1)
                    if p == L0 and first and jb % B == 0 and jb // B + 1 < GROUPS:
                        layer0_norm(jb // B + 1)
                        if jb // B + 2 < GROUPS:
                            layer0_stats(jb // B + 2)
                    if p == L0 and first and jb == BLOCKS - 2:
                        dve.wait_ge(w_in, 16 * 11)
                        nc.vector.tensor_tensor(bias_g[:, :], bias[:, 1:3], bias[:, 4:6], ALU.add).then_inc(bias_ready, 1)
                        dve.wait_ge(bias_ready, 1)
                        nc.vector.tensor_scalar(bias_g[:, :], bias_g[:, :], 0.5, None, ALU.mult).then_inc(bias_ready, 1)

            def weighted(g, jb):
                dve.wait_ge(w_made, g * BLOCKS + jb + B)
                if not (isinstance(g, int) and g * BLOCKS + jb < PBUFS):
                    dve.wait_ge(att_mm, g * BLOCKS + jb + B - PBUFS)
                w, q = jb % WBUFS, jb % PBUFS
                nc.vector.tensor_tensor(att_p[:, q + 1:q + B, :], att_w[:, w + 1:w + B, :], ring[:, (jb // B) % SLOTS, 1:B, :],
                                        ALU.mult).then_inc(p_made, B)

            def layer0_stats(k):
                dve.wait_ge(x_in[(k + 1) // 2], 16 if k in (0, GROUPS - 1) else 32)
                stats(k, lambda b: x_all[:, k * B + b, :])

            def layer0_norm(k):
                normalise(k, lambda b: x_all[:, k * B + b, :], nat_a[:, k * B:(k + 1) * B, :], k)

            layer0_stats(0)
            layer0_norm(0)
            layer0_stats(1)
            passes(dve, body)
            for jb in range(BLOCKS):
                tail3(GROUPS - 1, jb)

        @block.gpsimd
        def _(pool):
            g_ = nc.gpsimd
            g_.memset(ident[:, :], 0.0).then_inc(const_step, 1)
            pool.wait_ge(const_step, 1)
            g_.affine_select(out=ident[:, :], in_=ident[:, :], compare_op=ALU.not_equal, fill=1.0, base=0,
                             pattern=[[-1, P]], channel_multiplier=1).then_inc(const_ready, 1)
            g_.memset(avg32[:, :], 1.0 / 32)
            g_.memset(ones[:, :], 1.0)
            g_.memset(phalf[:, :], 0.5)
            g_.memset(ln_eps[:, :], LN_EPS)
            g_.memset(minus_one[:, :], -1.0)
            g_.memset(mhalf[:, :], -0.5).then_inc(const_ready, 1)
            pool.wait_ge(const_ready, 2)

            def chain(ins):
                pool.drain()

            def layer_rstd(c, chain, nbias_too=False):
                pool.wait_ge(ln_mv, c + 1)
                chain(g_.tensor_tensor(rstd[:, :], mv[:, :, 1], ln_eps[:, :], ALU.add))
                if nbias_too:
                    chain(g_.tensor_tensor(rstd[:, :], rstd[:, :], mhalf[:, 0:B], ALU.pow))
                    chain(g_.tensor_tensor(nbias[:, :], mv[:, :, 0], rstd[:, :], ALU.mult))
                    g_.tensor_scalar(nbias[:, :], nbias[:, :], -1.0, None, ALU.mult).then_inc(ln_rstd, 1)
                else:
                    g_.tensor_tensor(rstd[:, :], rstd[:, :], mhalf[:, 0:B], ALU.pow).then_inc(ln_rstd, 1)

            def split(p, k, chain):
                blk = slice(k * B, (k + 1) * B)
                nat = nat_b if p == L2 else nat_a
                if p == L2:
                    pool.wait_ge(den_mm, (GROUPS * BLOCKS - WBUFS + k) // B + 1)
                pool.wait_ge(hi_split, AGG[p] * GROUPS + k + 1)
                g_.tensor_tensor(src_lo[:, blk, :], nat[:, blk, :], src_hi[:, blk, :].bitcast(F32), ALU.subtract).then_inc(src_ready, 1)

            def scale_source(k):
                blk = slice(k * B, (k + 1) * B)
                pool.wait_ge(ln_done, 2 * GROUPS + k + 1)
                g_.tensor_tensor(nat_b[:, blk, :], nat_b[:, blk, :], wide(dinv[:, blk]), ALU.mult).then_inc(scaled_src, 1)

            def tail0(e, chain):
                layer_rstd(GROUPS + e, chain)

            def tail1(e, chain):
                layer_rstd(2 * GROUPS + e, chain, nbias_too=True)

            def ts(chain, dst, a, s1, s2, o1, o2=None):
                chain(g_.tensor_scalar(SC[dst], SC[a], s1, s2, o1, o2) if o2 is not None else
                      g_.tensor_scalar(SC[dst], SC[a], s1, None, o1))

            def tt(chain, dst, a, b, op):
                chain(g_.tensor_tensor(SC[dst], SC[a], SC[b], op))

            def divide(chain, dst, a, b):
                chain(g_.tensor_tensor(SC["rec"], SC[b], minus_one[:, :], ALU.pow))
                tt(chain, dst, a, "rec", ALU.mult)

            def artanh_arg(chain, src):
                ts(chain, "xc", src, 1.0 - EPS, -1.0 + EPS, ALU.min, ALU.max)
                ts(chain, "inv", "xc", -1.0, 1.0, ALU.mult, ALU.add)
                ts(chain, "one", "xc", 1.0, None, ALU.add)
                divide(chain, "arg", "one", "inv")

            def artanh_series(chain):
                tt(chain, "z2", "xc", "xc", ALU.mult)
                ts(chain, "ser", "z2", 1.0 / 7, 1.0 / 5, ALU.mult, ALU.add)
                tt(chain, "ser", "ser", "z2", ALU.mult)
                ts(chain, "ser", "ser", 1.0 / 3, None, ALU.add)
                tt(chain, "ser", "ser", "z2", ALU.mult)
                ts(chain, "ser", "ser", 1.0, None, ALU.add)
                tt(chain, "ser", "ser", "xc", ALU.mult)
                ts(chain, "mask", "xc", 1.0 / 16, None, ALU.is_lt)

            SC["half"] = phalf[:, :]

            def artanh_end(chain):
                tt(chain, "ath", "ln", "half", ALU.mult)
                tt(chain, "ser", "ser", "ath", ALU.subtract)
                tt(chain, "ser", "ser", "mask", ALU.mult)
                tt(chain, "ath", "ath", "ser", ALU.add)

            def tail2_norm(e, chain):
                layer_rstd(3 * GROUPS + e, chain)

            def tail2a(e, chain):
                pool.wait_ge(xn2_ready, e + 1)
                chain(g_.tensor_tensor(SC["xn"], SC["xn2"], phalf[:, :], ALU.pow))
                ts(chain, "xn", "xn", MIN_NORM, None, ALU.max)
                artanh_arg(chain, "xn")
                g_.tensor_copy(SC["arg"], SC["arg"]).then_inc(ln_arg, 1)

            def tail2b(e, chain):
                artanh_series(chain)
                pool.wait_ge(mx_ready, e + 1)
                chain(g_.tensor_tensor(SC["mxn"], SC["ss"], phalf[:, :], ALU.pow))
                ts(chain, "mxn", "mxn", MIN_NORM, None, ALU.max)
                divide(chain, "z", "mxn", "xn")
                pool.wait_ge(ln_val, e + 1)
                artanh_end(chain)
                tt(chain, "z", "z", "ath", ALU.mult)
                g_.tensor_copy(SC["z"], SC["z"]).then_inc(th_arg, 1)

            def tail2c(e, chain):
                pool.wait_ge(th_val, e + 1)
                divide(chain, "f", "t", "mxn")
                tt(chain, "g", "f", "f", ALU.mult)
                tt(chain, "g", "g", "ss", ALU.mult)
                ts(chain, "g", "g", -1.0, 1.0, ALU.mult, ALU.add)
                ts(chain, "g", "g", EPS, None, ALU.max)
                ts(chain, "g", "g", 0.5, None, ALU.mult)
                chain(g_.tensor_tensor(SC["g"], SC["g"], minus_one[:, :], ALU.pow))
                ts(chain, "c", "g", -1.0, None, ALU.add)
                g_.tensor_copy(cols(q_all, e), SC["c"]).then_inc(q_ready, 1)
                tt(chain, "f", "f", "g", ALU.mult)
                g_.tensor_tensor(grp(nat_a, e), y_nat[:, :, :], wide(SC["f"]), ALU.mult).then_inc(hyp_src_ready, 1)

            def add_den(g, jbs, chain):
                for jb in jbs:
                    i, n = POOL_DEN.index(jb), len(POOL_DEN)
                    if i == 0:
                        continue
                    pool.wait_ge(den_scaled_ready, g * n + i + 1)
                    a = den_scaled[:, 0, :] if i == 1 else pool_den[:, :]
                    total = pool_den_s if i == n - 1 else pool_den
                    chain(g_.tensor_tensor(total[:, :], a, den_scaled[:, i % DBUFS, :], ALU.add).then_inc(pool_den_added, 2 if i == 1 else 1))

            def tail3(e, chain, g=None):
                def add(jbs):
                    if g is not None:
                        add_den(g, jbs, chain)

                add(POOL_DEN[:5])
                pool.wait_ge(v_ready, e + 1)
                pool.wait_ge(den_ready, e + 1)
                chain(g_.tensor_tensor(SC["mxn"], SC["ss"], phalf[:, :], ALU.pow))
                ts(chain, "sgn", "den", 0.0, None, ALU.is_ge)
                ts(chain, "sgn", "sgn", 2.0, -1.0, ALU.mult, ALU.add)
                tt(chain, "den", "den", "sgn", ALU.mult)
                ts(chain, "den", "den", CLAMP, None, ALU.max)
                divide(chain, "xn", "mxn", "den")
                ts(chain, "xn", "xn", MIN_NORM, None, ALU.max)
                artanh_arg(chain, "xn")
                g_.tensor_copy(SC["arg"], SC["arg"]).then_inc(ln_arg3, 1)
                tt(chain, "den", "den", "xn", ALU.mult)
                artanh_series(chain)
                add(POOL_DEN[5:7])
                pool.wait_ge(ln_val3, e + 1)
                artanh_end(chain)
                ts(chain, "ath", "ath", 0.5, None, ALU.mult)
                chain(g_.tensor_tensor(SC["ath"], SC["ath"], cols(rowsum, e), ALU.mult))
                ts(chain, "ath", "ath", ATANH_MAX, -ATANH_MAX, ALU.min, ALU.max)
                divide(chain, "c", "ath", "den")
                g_.tensor_tensor(SC["c"], SC["c"], SC["sgn"], ALU.mult).then_inc(c_ready, 1)
                add(POOL_DEN[7:9])
                pool.wait_ge(un2_ready, e + 1)
                chain(g_.tensor_tensor(SC["un"], SC["ss"], phalf[:, :], ALU.pow))
                ts(chain, "un", "un", MIN_NORM, None, ALU.max)
                g_.tensor_copy(SC["un"], SC["un"]).then_inc(th_arg3, 1)
                add(POOL_DEN[9:10])
                pool.wait_ge(th_val3, e + 1)
                chain(g_.tensor_tensor(SC["rec"], SC["un"], minus_one[:, :], ALU.pow))
                g_.tensor_tensor(SC["k"], SC["t"], SC["rec"], ALU.mult).then_inc(k_ready, 1)
                add(POOL_DEN[10:])

            def tail2(e, chain):
                tail2_norm(e, chain)
                tail2a(e, chain)
                tail2b(e, chain)
                tail2c(e, chain)

            def looped(tail, count=GROUPS - 1):
                with pool.Fori(0, count) as e:
                    tail(e, chain)

            for k in range(GROUPS):
                layer_rstd(k, chain)
                split(L0, k, chain)
            with pool.Fori(0, GROUPS - 1) as e:
                tail0(e, chain)

            def weighted(g, jb):
                pool.wait_ge(w_made, g * BLOCKS + jb + 2)
                if not (isinstance(g, int) and g * BLOCKS + jb < PBUFS):
                    pool.wait_ge(att_mm, g * BLOCKS + jb + 1 - PBUFS)
                g_.tensor_tensor(att_p[:, jb % PBUFS, :], att_w[:, jb % WBUFS, :], ring[:, (jb // B) % SLOTS, 0, :],
                                 ALU.mult).then_inc(pool_p_made, B)

            def inv_sqrt_degree(k):
                blk = slice(k * B, (k + 1) * B)
                chain(g_.tensor_scalar(dinv[:, blk], rowsum[:, blk], 1.0, DEG_EPS, ALU.add, ALU.add))
                chain(g_.tensor_tensor(dinv[:, blk], dinv[:, blk], mhalf[:, 0:B], ALU.pow))
                scale_source(k)

            last = GROUPS - 1
            for jb in range(0, BLOCKS, B):
                if jb == 5 * B:
                    tail0(last, chain)
                weighted(0, jb)
            with pool.Fori(1, last) as g:
                for jb in range(0, BLOCKS, B):
                    if jb == 3 * B:
                        tail1(g - 1, chain)
                    weighted(g, jb)
            for jb in range(0, BLOCKS, B):
                if jb == 3 * B:
                    tail1(last - 1, chain)
                weighted(last, jb)
                if jb == 0:
                    pool.wait_ge(row_summed, last * BLOCKS)
                    pool.wait_ge(last_summed, GROUPS * B)
                    chain(g_.tensor_tensor(rowsum[:, :], deg_part[:, :, 0], deg_part[:, :, 1], ALU.add))
                    for i in range(2, TILES):
                        chain(g_.tensor_tensor(rowsum[:, :], rowsum[:, :], deg_part[:, :, i], ALU.add))
                else:
                    inv_sqrt_degree(jb // B - 1)
            for k in range(5):
                split(L2, k, chain)
            tail1(last, chain)
            for k in range(5, last):
                split(L2, k, chain)
            inv_sqrt_degree(last)
            split(L2, last, chain)
            looped(tail2)
            for k in range(3):
                split(L3, k, chain)
            add_den(0, POOL_DEN[:2], chain)
            tail2_norm(last, chain)
            split(L3, 3, chain)
            add_den(0, POOL_DEN[2:4], chain)
            for k in range(4, last):
                split(L3, k, chain)
            tail2a(last, chain)
            add_den(0, POOL_DEN[4:6], chain)
            tail2b(last, chain)
            add_den(0, POOL_DEN[6:8], chain)
            tail2c(last, chain)
            add_den(0, POOL_DEN[8:9], chain)
            split(L3, last, chain)
            add_den(0, POOL_DEN[9:], chain)
            with pool.Fori(1, GROUPS) as g:
                tail3(g - 1, chain, g)
            tail3(GROUPS - 1, chain)


_INS = ['x', 'adj', 'L0_gnn_W_msg', 'L0_gnn_b_msg', 'L0_gnn_W_ih', 'L0_gnn_W_hh', 'L0_gnn_b_ih', 'L0_gnn_b_hh',
        'L1_gnn_weight', 'L1_gnn_att_src', 'L1_gnn_att_dst', 'L2_gnn_weight', 'L3_gnn_W']
_OUTS = [((4096, 128), 'float32')]


def kernel(**inputs):
    import numpy as _np
    import concourse.bacc as _bacc
    from concourse import mybir as _mybir
    from concourse.bass_utils import run_bass_kernel_spmd as _run

    nc = _bacc.Bacc("TRN2", target_bir_lowering=False, num_devices=1)
    arrays, args = {}, []
    for name in _INS:
        a = _np.ascontiguousarray(inputs[name])
        arrays[f"in_{name}_dram"] = a
        args.append(nc.dram_tensor(f"in_{name}_dram", a.shape, _mybir.dt.from_np(a.dtype), kind="ExternalInput").ap())
    for i, (shape, dtype) in enumerate(_OUTS):
        dt = _mybir.dt.from_np(_np.dtype(dtype))
        args.append(nc.dram_tensor(f"out_{i}_dram", shape, dt, kind="ExternalOutput").ap())
    adjacency_stack(nc, *args)
    r = _run(nc, [arrays], core_ids=[0])
    return r.results[0]["out_0_dram"]
```
